# Optimizing a Trainium2 kernel written in Bass

```python
import numpy as np
import jax
import jax.numpy as jnp

def _softmax(x, axis=-1):
    return jax.nn.softmax(x, axis=axis)

def _gelu(x):
    return jax.nn.gelu(x, approximate=True)

def _silu(x):
    return jax.nn.silu(x)

def _sigmoid(x):
    return jax.nn.sigmoid(x)

def _layernorm(x, axis=-1, eps=1e-05):
    m = jnp.mean(x, axis=axis, keepdims=True)
    v = jnp.var(x, axis=axis, keepdims=True)
    return (x - m) / jnp.sqrt(v + eps)

def _scatter_add(tgt, idx, src, axis=0):
    return tgt.at[idx].add(src)

def _segment_sum(src, seg, n):
    return jax.ops.segment_sum(src, seg, n)
kernel_name = 'mk_hybrid_d1_jaxref_r4_5c5912'

def setup_inputs(seed: int=0):
    np.random.seed(seed)
    _w = jnp.asarray

    def _L0_attn_a_setup():
        import jax, jax.numpy as jnp
        import numpy as np
        B_, L_, DM, DIN, N_, K_, R_ = (1, 256, 256, 512, 16, 4, 64)
        key = jax.random.key(seed)
        ks = jax.random.split(key, 10)
        rn = lambda k, shape, s: jax.random.normal(k, shape, jnp.float32) * s
        dt_min, dt_max = (0.001, 0.1)
        u = jax.random.uniform(ks[6], (DIN,), jnp.float32)
        dt = jnp.exp(u * (np.log(dt_max) - np.log(dt_min)) + np.log(dt_min))
        b_dt = dt + jnp.log(-jnp.expm1(-dt))
        A_log = jnp.log(jnp.broadcast_to(jnp.arange(1, N_ + 1, dtype=jnp.float32), (DIN, N_)))
        return {'x': rn(ks[0], (B_, L_, DM), 1.0), 'W_in': rn(ks[1], (2 * DIN, DM), 0.02), 'conv_w': rn(ks[2], (DIN, K_), 0.1), 'conv_b': rn(ks[3], (DIN,), 0.02), 'W_x': rn(ks[4], (R_ + 2 * N_, DIN), 0.02), 'W_dt': rn(ks[5], (DIN, R_), R_ ** (-0.5)), 'b_dt': b_dt, 'A_log': A_log, 'D_param': jnp.ones((DIN,), jnp.float32), 'W_out': rn(ks[7], (DM, DIN), 0.02)}
    _L0_attn_a_in = _L0_attn_a_setup()

    def _L0_attn_b_setup():
        import math
        import jax, jax.numpy as jnp
        import numpy as np
        N, T, C = (4, 512, 256)
        H, HS = (16, 64)
        LAYER_ID, N_LAYERS = (1, 12)
        _EPS = math.exp(-LAYER_ID / N_LAYERS)
        EPS_R = _EPS / 2.0
        EPS_K = _EPS + 0.3 * LAYER_ID / (N_LAYERS - 1)
        EPS_V = _EPS

        def _time_interp(x, eps):
            Tn = x.shape[1]
            curr = jnp.pad(x, ((0, 0), (1, 0), (0, 0)))[:, :Tn]
            prev = jnp.pad(x, ((0, 0), (0, 1), (0, 0)))[:, 1:]
            return eps * curr + (1.0 - eps) * prev
        key = jax.random.key(seed)
        ks = jax.random.split(key, 9)
        s = 1.0 / math.sqrt(C)
        return {'x': jax.random.normal(ks[0], (N, T, C), dtype=jnp.float32), 'Wr': jax.random.normal(ks[1], (H * HS, C), dtype=jnp.float32) * s, 'br': jax.random.normal(ks[2], (H * HS,), dtype=jnp.float32) * 0.01, 'Wk': jax.random.normal(ks[3], (H * HS, C), dtype=jnp.float32) * s, 'bk': jax.random.normal(ks[4], (H * HS,), dtype=jnp.float32) * 0.01, 'Wv': jax.random.normal(ks[5], (H * HS, C), dtype=jnp.float32) * s, 'bv': jax.random.normal(ks[6], (H * HS,), dtype=jnp.float32) * 0.01, 'Wo': jax.random.normal(ks[7], (C, H * HS), dtype=jnp.float32) * s, 'bo': jax.random.normal(ks[8], (C,), dtype=jnp.float32) * 0.01, 'time_decay': jnp.full((H * HS,), 0.1, dtype=jnp.float32), 'U': jnp.full((H * HS,), 0.1, dtype=jnp.float32)}
    _L0_attn_b_in = _L0_attn_b_setup()

    def _L0_ffn_setup():
        import jax, jax.numpy as jnp
        import numpy as np
        DIM = 256
        HIDDEN = 768
        SCALE = 1.0 / 127.0

        def _dequant(w_int, dtype):
            return w_int.astype(dtype) * jnp.asarray(SCALE, dtype)
        key = jax.random.key(seed)
        k_x, k_g, k_u, k_d = jax.random.split(key, 4)
        x = jax.random.normal(k_x, (4, 512, DIM), dtype=jnp.float32)
        w_gate = jax.random.randint(k_g, (HIDDEN, DIM), -127, 128, dtype=jnp.int32)
        w_up = jax.random.randint(k_u, (HIDDEN, DIM), -127, 128, dtype=jnp.int32)
        w_down = jax.random.randint(k_d, (DIM, HIDDEN), -127, 128, dtype=jnp.int32)
        return {'x': x, 'w_gate': w_gate, 'w_up': w_up, 'w_down': w_down}
    _L0_ffn_in = _L0_ffn_setup()
    _d = {'L0_attn_a_x': _L0_attn_a_in['x'], 'L0_attn_a_W_in': _L0_attn_a_in['W_in'], 'L0_attn_a_conv_w': _L0_attn_a_in['conv_w'], 'L0_attn_a_conv_b': _L0_attn_a_in['conv_b'], 'L0_attn_a_W_x': _L0_attn_a_in['W_x'], 'L0_attn_a_W_dt': _L0_attn_a_in['W_dt'], 'L0_attn_a_b_dt': _L0_attn_a_in['b_dt'], 'L0_attn_a_A_log': _L0_attn_a_in['A_log'], 'L0_attn_a_D_param': _L0_attn_a_in['D_param'], 'L0_attn_a_W_out': _L0_attn_a_in['W_out'], 'L0_attn_b_Wr': _L0_attn_b_in['Wr'], 'L0_attn_b_br': _L0_attn_b_in['br'], 'L0_attn_b_Wk': _L0_attn_b_in['Wk'], 'L0_attn_b_bk': _L0_attn_b_in['bk'], 'L0_attn_b_Wv': _L0_attn_b_in['Wv'], 'L0_attn_b_bv': _L0_attn_b_in['bv'], 'L0_attn_b_Wo': _L0_attn_b_in['Wo'], 'L0_attn_b_bo': _L0_attn_b_in['bo'], 'L0_attn_b_time_decay': _L0_attn_b_in['time_decay'], 'L0_attn_b_U': _L0_attn_b_in['U'], 'L0_ffn_w_gate': _L0_ffn_in['w_gate'], 'L0_ffn_w_up': _L0_ffn_in['w_up'], 'L0_ffn_w_down': _L0_ffn_in['w_down']}
    _x0 = _d['L0_attn_a_x']
    _d['L0_attn_a_x'] = jax.random.normal(jax.random.fold_in(jax.random.key(seed), 1), (8, 512, 256), dtype=_x0.dtype)
    del _x0
    return _d

def reference(L0_attn_a_x, L0_attn_a_W_in, L0_attn_a_conv_w, L0_attn_a_conv_b, L0_attn_a_W_x, L0_attn_a_W_dt, L0_attn_a_b_dt, L0_attn_a_A_log, L0_attn_a_D_param, L0_attn_a_W_out, L0_attn_b_Wr, L0_attn_b_br, L0_attn_b_Wk, L0_attn_b_bk, L0_attn_b_Wv, L0_attn_b_bv, L0_attn_b_Wo, L0_attn_b_bo, L0_attn_b_time_decay, L0_attn_b_U, L0_ffn_w_gate, L0_ffn_w_up, L0_ffn_w_down):

    def _L0_attn_a_ref(x, W_in, conv_w, conv_b, W_x, W_dt, b_dt, A_log, D_param, W_out):
        import jax, jax.numpy as jnp
        import numpy as np
        B_, L_, DM, DIN, N_, K_, R_ = (1, 256, 256, 512, 16, 4, 64)
        Din, K = conv_w.shape
        R = W_dt.shape[1]
        N = A_log.shape[1]
        xz = jnp.einsum('bld,ed->ble', x, W_in)
        xs, z = jnp.split(xz, 2, axis=-1)
        xt = jnp.transpose(xs, (0, 2, 1))
        xc = jax.lax.conv_general_dilated(xt, conv_w[:, None, :], (1,), [(K - 1, 0)], feature_group_count=Din)
        xc = jnp.transpose(xc, (0, 2, 1)) + conv_b
        xc = jax.nn.silu(xc)
        x_dbl = jnp.einsum('bld,ed->ble', xc, W_x)
        dt, Bm, Cm = jnp.split(x_dbl, [R, R + N], axis=-1)
        dt = jax.nn.softplus(jnp.einsum('blr,dr->bld', dt, W_dt) + b_dt)
        A = -jnp.exp(A_log)
        A_bar = jnp.exp(dt[..., None] * A)
        Bu = dt[..., None] * Bm[:, :, None, :] * xc[..., None]

        def comb(e1, e2):
            a1, b1 = e1
            a2, b2 = e2
            return (a2 * a1, a2 * b1 + b2)
        _, h_all = jax.lax.associative_scan(comb, (A_bar, Bu), axis=1)
        y = jnp.einsum('bldn,bln->bld', h_all, Cm) + D_param * xc
        y = y * jax.nn.silu(z)
        return jnp.einsum('bld,ed->ble', y, W_out)

    def _L0_attn_b_ref(x, Wr, br, Wk, bk, Wv, bv, Wo, bo, time_decay, U):
        import math
        import jax, jax.numpy as jnp
        import numpy as np
        N, T, C = (4, 512, 256)
        H, HS = (16, 64)
        LAYER_ID, N_LAYERS = (1, 12)
        _EPS = math.exp(-LAYER_ID / N_LAYERS)
        EPS_R = _EPS / 2.0
        EPS_K = _EPS + 0.3 * LAYER_ID / (N_LAYERS - 1)
        EPS_V = _EPS

        def _time_interp(x, eps):
            Tn = x.shape[1]
            curr = jnp.pad(x, ((0, 0), (1, 0), (0, 0)))[:, :Tn]
            prev = jnp.pad(x, ((0, 0), (0, 1), (0, 0)))[:, 1:]
            return eps * curr + (1.0 - eps) * prev
        n, t, c = x.shape
        R = (_time_interp(x, EPS_R) @ Wr.T + br).reshape(n, t, H, HS)
        K = (_time_interp(x, EPS_K) @ Wk.T + bk).reshape(n, t, H, HS)
        V = (_time_interp(x, EPS_V) @ Wv.T + bv).reshape(n, t, H, HS)
        w = jax.nn.relu(time_decay).reshape(1, 1, H, HS)
        t_rem = (t - jnp.arange(1, t + 1, dtype=x.dtype)).reshape(1, t, 1, 1)
        W = -w * t_rem
        e = jnp.exp(jnp.clip(W + K, -20.0, 10.0))
        past_attention = jnp.cumsum(e * V, axis=1)
        past_energy = jnp.cumsum(e, axis=1)
        shift = lambda a: jnp.pad(a, ((0, 0), (1, 0), (0, 0), (0, 0)))[:, :t]
        eu = jnp.exp(jnp.clip(U.reshape(1, 1, H, HS) + K, -20.0, 10.0))
        A = shift(past_attention) + eu * V
        B = shift(past_energy) + eu
        WKV = A / B
        out = (jax.nn.sigmoid(R) * WKV).reshape(n, t, -1) @ Wo.T + bo
        return out

    def _L0_ffn_ref(x, w_gate, w_up, w_down):
        import jax, jax.numpy as jnp
        import numpy as np
        DIM = 256
        HIDDEN = 768
        SCALE = 1.0 / 127.0

        def _dequant(w_int, dtype):
            return w_int.astype(dtype) * jnp.asarray(SCALE, dtype)
        wg = _dequant(w_gate, x.dtype)
        wu = _dequant(w_up, x.dtype)
        wd = _dequant(w_down, x.dtype)
        gate = jnp.einsum('bsd,hd->bsh', x, wg)
        up = jnp.einsum('bsd,hd->bsh', x, wu)
        h = jax.nn.silu(gate) * up
        return jnp.einsum('bsh,dh->bsd', h, wd)
    x = L0_attn_a_x
    x = x + _L0_attn_a_ref(_layernorm(x, axis=-1), L0_attn_a_W_in, L0_attn_a_conv_w, L0_attn_a_conv_b, L0_attn_a_W_x, L0_attn_a_W_dt, L0_attn_a_b_dt, L0_attn_a_A_log, L0_attn_a_D_param, L0_attn_a_W_out)
    x = x + _L0_ffn_ref(_layernorm(x, axis=-1), L0_ffn_w_gate, L0_ffn_w_up, L0_ffn_w_down)
    x = x + _L0_attn_b_ref(_layernorm(x, axis=-1), L0_attn_b_Wr, L0_attn_b_br, L0_attn_b_Wk, L0_attn_b_bk, L0_attn_b_Wv, L0_attn_b_bv, L0_attn_b_Wo, L0_attn_b_bo, L0_attn_b_time_decay, L0_attn_b_U)
    x = x + _L0_ffn_ref(_layernorm(x, axis=-1), L0_ffn_w_gate, L0_ffn_w_up, L0_ffn_w_down)
    return x

_drawn_inputs = setup_inputs


def setup_inputs(seed=0):
    import zlib

    import numpy as np

    out = dict(_drawn_inputs(seed))
    spreads = {'L0_attn_a_D_param': (1.0, 0.2),
     'L0_attn_b_time_decay': (0.10000000149011612, 0.2),
     'L0_attn_b_U': (0.10000000149011612, 0.2)}
    factors = {}
    for name, (base, spread) in spreads.items():
        noise = np.random.default_rng([zlib.crc32(name.encode()), seed]).standard_normal(out[name].shape)
        drawn = base * np.exp(spread * noise) if base else spread * noise
        out[name] = jnp.asarray(drawn.astype(out[name].dtype))
    for name, factor in factors.items():
        out[name] = (out[name] * factor).astype(out[name].dtype)
    return out
```

```python
import numpy as np
import concourse.bass as bass
from concourse import mybir
from contextlib import ExitStack

NSEQ, T, C = 8, 512, 256
DIN, NST, TAPS, RANK = 512, 16, 4, 64
HID = 768
ATT = 1024
P = 128
KC, JD, FM, CT, TT = C // P, DIN // P, HID // P, ATT // P, T // P
EPS_LN = 1e-5
EPS = float(np.exp(-1 / 12))
MIX = (EPS / 2.0, EPS + 0.3 / 11, EPS)
LO, HI = -20.0, 10.0
PC = {}
_at = 0
for _n, _w in (("conv_w", JD * TAPS), ("conv_b", JD), ("b_dt", JD), ("A_log", JD * NST), ("D", JD),
               ("br", CT), ("bk", CT), ("bv", CT), ("decay", CT), ("U", CT)):
    PC[_n] = _at
    _at += _w
NPAR = _at

STEPS = JD // 2 * NST
M_HEAD = ([("m_norm", 0)] + [("m_in", m) for m in range(2 * JD)] + [("m_conv", k) for k in range(TAPS)]
          + [("m_xproj", 0)])
M_DT = [("m_dt", j) for j in range(JD)]
M_SCAN = []
for _jp in range(JD // 2):
    M_SCAN += [("m_step", _jp * NST + n) for n in range(NST)] + [("m_gate", _jp)]
M_POST = [("m_post", 0)]
FFN1 = [("r_norm", 0)] + [("r_up", m) for m in range(FM)] + [("r_down", h) for h in range(2)]
MIXING = [("r_norm", 1), ("r_mix", 0)]
RECEPT = [("r_recept", c) for c in range(CT)]
KV = [("r_kv", c) for c in range(CT)] + [("r_kvlast", 0)] + [("r_wo", h) for h in range(2)]
FFN2 = [("r_norm", 2)] + [("r_up", FM + m) for m in range(FM)] + [("r_down", 2 + h) for h in range(2)]
WEIGHT = {"m_norm": 3, "m_in": 2, "m_conv": 2.5, "m_xproj": 6, "m_dt": 3, "m_step": 3.2, "m_gate": 2.5,
          "r_norm": 3, "r_up": 3.4, "r_down": 5, "r_mix": 5, "r_recept": 1.7, "r_kv": 8, "r_kvlast": 2, "r_wo": 7}


def merged(a, b):
    ta, tb = (sum(WEIGHT[k] for k, _ in x) for x in (a, b))
    out, i, j, da, db = [], 0, 0, 0.0, 0.0
    while i < len(a) or j < len(b):
        if j == len(b) or (i < len(a) and da / ta <= db / tb):
            da += WEIGHT[a[i][0]]
            out.append(a[i])
            i += 1
        else:
            db += WEIGHT[b[j][0]]
            out.append(b[j])
            j += 1
    return out


MAMBA = M_HEAD + M_DT + M_SCAN + M_POST
REST = FFN1 + MIXING + RECEPT + KV + FFN2
BOTH = (merged(FFN1, M_HEAD) + merged(MIXING, M_DT) + merged(RECEPT + KV + FFN2, M_SCAN) + M_POST)


def gate_banks():
    uses, n = {}, 0
    for unit, i in REST:
        if unit == "r_up":
            uses[i] = n
        n += {"r_norm": KC, "r_up": 1, "r_recept": 1, "r_kv": 2}.get(unit, 0)
    return uses


GATE_BANK = gate_banks()


class Signal:

    def __init__(self, sem, per, first=0):
        self.sem, self.per, self.first = sem, per, first


def at(signal, seq, count):
    return seq * signal.per + (signal.first + count)


def hybrid_block(nc, x, w_in, w_x, w_dt, w_out, w_gate, w_up, w_down, w_r, w_k, w_v, w_o, b_o, params,
                 ident_in, steps_left, out):
    f32, bf16, i32 = mybir.dt.float32, mybir.dt.bfloat16, mybir.dt.int32
    ALU, ACT = mybir.AluOpType, mybir.ActivationFunctionType
    x_v = x.rearrange("s (t p) c -> s p t c", p=P)
    out_v = out.rearrange("s (t p) c -> s p t c", p=P)

    with ExitStack() as ctx:
        def sb(name, shape, dt=f32):
            return ctx.enter_context(nc.sbuf_tensor(name, shape, dt))

        def bank(name):
            return ctx.enter_context(nc.psum_tensor(name, [P, T], f32))

        def signal(name, per, first=0):
            return Signal(ctx.enter_context(nc.semaphore(name)), per, first)

        win = sb("win", [P, KC, 2 * DIN])
        wx_dt = sb("wx_dt", [P, JD, RANK])
        wx_bc = sb("wx_bc", [P, JD, 3, 2 * NST])
        wdt = sb("wdt", [RANK, DIN])
        wout = sb("wout", [P, JD, C])
        wgate = sb("wgate", [P, KC, HID])
        wup = sb("wup", [P, KC, HID])
        wdown = sb("wdown", [P, FM, C])
        wr, wk, wv = (sb(n, [P, KC, ATT]) for n in ("wr", "wk", "wv"))
        wo = sb("wo", [P, CT, C])
        bo = sb("bo", [1, C])
        par = sb("par", [P, NPAR])
        neg_a = sb("neg_a", [P, JD * NST])
        neg_w = sb("neg_w", [P, CT])
        ubk = sb("ubk", [P, CT])
        half_br = sb("half_br", [P, CT])
        ident = sb("ident", [P, P])
        select = sb("select", [3 * 2 * NST, 2 * NST, P], bf16)
        t_left = sb("t_left", [P, T])
        ones = sb("ones", [P, P])
        minus_half = sb("minus_half", [P, TT])

        xin = sb("xin", [P, TT, C])
        xs = sb("xs", [P, JD, T + TAPS - 1])
        xc = sb("xc", [P, JD, T])
        sz = sb("sz", [P, JD, T])
        dtx = sb("dtx", [P, JD, T])
        u1 = sb("u1", [P, 2, T])
        bcf = u1[0:3 * 2 * NST, 0, :]
        bc3 = sb("bc3", [3 * 2 * NST, T], bf16)
        b_all = sb("b_all", [P, 3, T])
        decay = sb("decay", [P, 4, T])
        xnT = decay[:, 0:KC, :]
        dtr = b_all[0:RANK, 0, :]
        bu = sb("bu", [P, 2, T])
        h = sb("h", [P, 3, T])
        hc = sb("hc", [P, 4, T])
        dt = xs[:, :, TAPS - 1:]

        xr = sb("xr", [P, TT, C])
        xT = sb("xT", [P, KC, T + 2])
        mix = sb("mix", [P, 3, KC, T])
        hf = mix[:, :, :, :].rearrange("p a k t -> p (a k) t")
        yr = sb("yr", [P, CT, T])
        kv = sb("kv", [P, 4, T])
        ek, vv, eu, ev = (kv[:, i, :] for i in range(4))
        xnr = kv[:, 0:2, :].rearrange("p a (t c) -> p (a t) c", c=C)
        xout = kv[:, 2:4, :].rearrange("p a (t c) -> p (a t) c", c=C)
        sums = sb("sums", [P, 2, T + 1])
        sg = sums[:, :, 1:]
        num, den, rec = (sb(n, [P, T]) for n in ("num", "den", "rec"))

        stats = {f: sb(f + "_stats", [P, TT, 6]) for f in "mr"}
        moments = {f: sb(f + "_moments", [P, TT, 2]) for f in "mr"}
        var_eps = {f: sb(f + "_var_eps", [P, TT]) for f in "mr"}
        rstd = {f: sb(f + "_rstd", [P, TT]) for f in "mr"}

        ps_m = bank("ps_m")
        ps_c = [bank(f"ps_c{i}") for i in range(2)]
        ps_y = [bank(f"ps_y{i}") for i in range(2)]
        ps_r = [bank(f"ps_r{i}") for i in range(2)]
        ps_v = bank("ps_v")

        weights_in = signal("weights_in", 0)
        par_in = signal("par_in", 0)
        ffn_in = signal("ffn_in", 0)
        pool_const = signal("pool_const", 0)
        setup_act = signal("setup_act", 0)
        setup_dve = signal("setup_dve", 0)
        carried = signal("carried", 0)
        x_loaded = signal("x_loaded", 32)
        out_stored = signal("out_stored", 16, first=16)
        n_stats = {"m": signal("m_stat", TT), "r": signal("r_stat", 3 * TT)}
        n_moments = {"m": signal("m_mom", TT), "r": signal("r_mom", 3 * TT)}
        n_var = {"m": signal("m_var", 1), "r": signal("r_var", 3)}
        n_rstd = {"m": signal("m_rstd_done", 1), "r": signal("r_rstd_done", 3)}
        n_normed = {"m": signal("m_normed", 1), "r": signal("r_normed", 3)}
        n_turned = {"m": signal("m_turned", KC), "r": signal("r_turned", 3 * KC)}
        m_full = signal("m_full", KC + 2 * JD + 2 + JD + STEPS)
        xs_ready = signal("xs_ready", JD)
        sz_ready = signal("sz_ready", JD)
        conv_tap = signal("conv_tap", JD * TAPS)
        xc_ready = signal("xc_ready", JD)
        dtr_ready = signal("dtr_ready", 1)
        bcf_ready = signal("bcf_ready", 1)
        bc_split = signal("bc_split", 5)
        sp_abs = signal("sp_abs", JD)
        sp_relu = signal("sp_relu", JD)
        sp_exp = signal("sp_exp", JD)
        sp_u = signal("sp_u", JD)
        sp_rest = signal("sp_rest", JD)
        sp_sum = signal("sp_sum", JD)
        sp_ln = signal("sp_ln", JD)
        dt_ready = signal("dt_ready", JD)
        dtx_ready = signal("dtx_ready", JD)
        b_ready = signal("b_ready", STEPS)
        decay_ready = signal("decay_ready", 2 * STEPS)
        bu_ready = signal("bu_ready", 2 * STEPS)
        scanned = signal("scanned", 2 * STEPS)
        hc_ready = signal("hc_ready", 2 * STEPS)
        y_added = signal("y_added", 2 * STEPS)
        c_full = signal("c_full", STEPS + 2)
        y_read = signal("y_read", JD)
        gated = signal("gated", JD)
        m_done = signal("m_done", 2)
        r_full = signal("r_full", 3 * KC + 2 * FM + 3 * CT)
        v_full = signal("v_full", 2 * FM + 6)
        v_read = signal("v_read", 2 * FM + 6)
        sg_ready = signal("sg_ready", 2 * FM)
        gate_read = signal("gate_read", FM)
        mix_scaled = signal("mix_scaled", 3 * KC)
        mix_ready = signal("mix_ready", 3 * KC)
        recept_ready = signal("recept_ready", CT)
        kb_ready = signal("kb_ready", CT)
        eu_ready = signal("eu_ready", CT)
        vv_ready = signal("vv_ready", CT)
        k_decayed = signal("k_decayed", CT)
        k_clipped = signal("k_clipped", CT)
        e_ready = signal("e_ready", CT)
        eu_clipped = signal("eu_clipped", CT)
        ev_ready = signal("ev_ready", CT)
        euv_ready = signal("euv_ready", CT)
        den_ready = signal("den_ready", CT)
        e_summed = signal("e_summed", CT)
        ev_summed = signal("ev_summed", CT)
        num_ready = signal("num_ready", CT)
        ln_ready = signal("ln_ready", CT)
        rec_ready = signal("rec_ready", CT)
        newton = signal("newton", 3 * CT)
        wkv_ready = signal("wkv_ready", CT)

        def col(name, i):
            return par[:, PC[name] + i:PC[name] + i + 1]

        def channel_tile(s):
            return 2 * (s // (2 * NST)) + s % 2

        def sequences(engine, run):
            run(MAMBA, 0, None)
            with engine.Fori(0, NSEQ - 1) as b:
                run(BOTH, b + 1, b)
            run(REST, None, NSEQ - 1)

        block = ctx.enter_context(nc.Block())

        @block.sync
        def _(sp):
            sp.sem_inc(out_stored.sem, 16)
            sp.dma_start(xin[:, :, :], x_v[0]).then_inc(x_loaded.sem, 16)
            sp.dma_start(par[:, :], params).then_inc(par_in.sem, 16)
            kp = "(k p) n -> p k n"
            sp.dma_start(ident[:, :], ident_in).then_inc(par_in.sem, 16)
            for dst, src in ((win[:, :, :], w_in.rearrange(kp, p=P)),
                             (wx_dt[:, :, :], w_x[:, 0:RANK].rearrange(kp, p=P)),
                             (wx_bc[:, :, 0, :], w_x[:, RANK:].rearrange(kp, p=P)),
                             (wx_bc[:, :, 1, :], w_x[:, RANK:].rearrange(kp, p=P)),
                             (wx_bc[:, :, 2, :], w_x[:, RANK:].rearrange(kp, p=P)),
                             (wdt[:, :], w_dt),
                             (wout[:, :, :], w_out.rearrange(kp, p=P)),
                             (wr[:, :, :], w_r.rearrange(kp, p=P)),
                             (wk[:, :, :], w_k.rearrange(kp, p=P)),
                             (wv[:, :, :], w_v.rearrange(kp, p=P)),
                             (wo[:, :, :], w_o.rearrange(kp, p=P)),
                             (bo[:, :], b_o)):
                sp.dma_start(dst, src).then_inc(weights_in.sem, 16)
            for dst, src in ((wgate, w_gate), (wup, w_up), (wdown, w_down)):
                sp.dma_start(dst[:, :, :].bitcast(i32), src.rearrange(kp, p=P)).then_inc(ffn_in.sem, 16)
            sp.dma_start(t_left[:, :], steps_left.to_broadcast([P, T])).then_inc(ffn_in.sem, 16)

            def reload(m):
                sp.wait_ge(n_turned["m"].sem, at(n_turned["m"], m, KC))
                sp.dma_start(xin[:, :, :], x_v[m]).then_inc(x_loaded.sem, 16)

            reload(0)
            with sp.Fori(0, NSEQ - 1) as b:
                sp.wait_ge(m_done.sem, at(m_done, b, 2))
                sp.dma_start(xin[:, :, :], x_v[b + 1]).then_inc(x_loaded.sem, 16)
                reload(b + 1)
                sp.wait_ge(v_read.sem, at(v_read, b, v_read.per))
                sp.dma_start(out_v[b], xout).then_inc(out_stored.sem, 16)
            sp.wait_ge(v_read.sem, at(v_read, NSEQ - 1, v_read.per))
            sp.dma_start(out_v[NSEQ - 1], xout).then_inc(out_stored.sem, 16)
            sp.wait_ge(out_stored.sem, at(out_stored, NSEQ - 1, 16))

        @block.gpsimd
        def _(pool):
            pool.memset(select[:, :, :], 0.0).then_inc(pool_const.sem, 1)
            pool.memset(minus_half[:, :], -0.5).then_inc(pool_const.sem, 1)
            pool.memset(ones[:, :], 1.0).then_inc(pool_const.sem, 1)
            pool.memset(xs[:, :, 0:TAPS - 1], 0.0).then_inc(pool_const.sem, 1)
            pool.memset(xT[:, :, 0:1], 0.0).then_inc(pool_const.sem, 1)
            pool.memset(xT[:, :, T + 1:T + 2], 0.0).then_inc(pool_const.sem, 1)
            pool.memset(sums[:, :, 0:1], 0.0).then_inc(pool_const.sem, 1)
            pool.wait_ge(pool_const.sem, 7)
            for part in range(3):
                rows = select[2 * NST * part:2 * NST * (part + 1), :, :]
                pool.affine_select(out=rows, in_=rows, compare_op=ALU.not_equal, fill=1.0, base=0,
                                   pattern=[[-1, 2 * NST], [0, P]], channel_multiplier=1)\
                    .then_inc(pool_const.sem, 1)
            pool.wait_ge(pool_const.sem, 10)

            def norm(f, seq, i):
                pool.wait_ge(n_var[f].sem, at(n_var[f], seq, i + 1))
                pool.tensor_tensor(rstd[f][:, :], var_eps[f][:, :], minus_half[:, :], ALU.pow)\
                    .then_inc(n_rstd[f].sem, 1)

            def inputs(m, i):
                pool.wait_ge(b_ready.sem, at(b_ready, m, i + 1))
                for s in (2 * i, 2 * i + 1):
                    if s >= 2:
                        pool.wait_ge(scanned.sem, at(scanned, m, s - 1))
                    pool.tensor_tensor(bu[:, s % 2, :], dtx[:, channel_tile(s), :], b_all[:, i % 3, :],
                                       ALU.mult).then_inc(bu_ready.sem, 1)

            def run(units, m, r):
                for unit, i in units:
                    if unit == "m_norm":
                        norm("m", m, 0)
                    elif unit == "r_norm":
                        norm("r", r, i)
                    elif unit == "m_dt":
                        pool.wait_ge(dt_ready.sem, at(dt_ready, m, i + 1))
                        pool.tensor_tensor(dtx[:, i, :], dt[:, i, :], xc[:, i, :], ALU.mult)\
                            .then_inc(dtx_ready.sem, 1)
                    elif unit == "m_step":
                        if i == 0:
                            pool.wait_ge(dtx_ready.sem, at(dtx_ready, m, JD))
                            inputs(m, 0)
                        if i + 1 < STEPS:
                            inputs(m, i + 1)
                    elif unit == "r_mix":
                        pool.wait_ge(n_turned["r"].sem, at(n_turned["r"], r, 2 * KC))
                        pool.sem_inc(carried.sem, 1)
                        for q in range(3):
                            for k in range(KC):
                                pool.tensor_scalar(mix[:, q, k, :], xT[:, k, 0:T], MIX[q], 1.0, ALU.mult, ALU.mult)\
                                    .then_inc(mix_scaled.sem, 1)
                    elif unit == "r_kv":
                        pool.wait_ge(eu_ready.sem, at(eu_ready, r, i + 1))
                        pool.sem_inc(carried.sem, 1)
                        pool.tensor_scalar(eu, eu, float(np.exp(np.float32(HI))), float(np.exp(np.float32(LO))),
                                           ALU.min, ALU.max).then_inc(eu_clipped.sem, 1)
                        pool.wait_ge(vv_ready.sem, at(vv_ready, r, i + 1))
                        pool.wait_ge(eu_clipped.sem, at(eu_clipped, r, i + 1))
                        if i:
                            pool.wait_ge(wkv_ready.sem, at(wkv_ready, r, i))
                        pool.tensor_tensor(num[:, :], eu, vv, ALU.mult).then_inc(euv_ready.sem, 1)
                        pool.wait_ge(e_ready.sem, at(e_ready, r, i + 1))
                        pool.tensor_tensor(ev, ek, vv, ALU.mult).then_inc(ev_ready.sem, 1)
                        pool.wait_ge(e_summed.sem, at(e_summed, r, i + 1))
                        pool.tensor_tensor(den[:, :], sums[:, 0, 0:T], eu, ALU.add).then_inc(den_ready.sem, 1)

            sequences(pool, run)

        @block.scalar
        def _(act):
            act.wait_ge(par_in.sem, 32)
            a0 = PC["A_log"]
            act.activation(neg_a[:, :], par[:, a0:a0 + JD * NST], ACT.Exp).then_inc(setup_act.sem, 1)
            act.wait_ge(pool_const.sem, 7)
            act.wait_ge(setup_dve.sem, 7)

            def turned(f, seq, i, src, full, first, dst):
                for k in range(KC):
                    act.wait_ge(full.sem, at(full, seq, first + k + 1))
                    act.copy(dst[k], src[k][:, :]).then_inc(n_turned[f].sem, 1)

            def reciprocal(r, c):
                act.wait_ge(den_ready.sem, at(den_ready, r, c + 1))
                act.activation(rec[:, :], den[:, :], ACT.Ln).then_inc(ln_ready.sem, 1)
                act.wait_ge(ln_ready.sem, at(ln_ready, r, c + 1))
                act.activation(rec[:, :], rec[:, :], ACT.Exp, scale=-1.0).then_inc(rec_ready.sem, 1)

            def copy_b(m, i, src):
                if i >= 3:
                    act.wait_ge(bu_ready.sem, at(bu_ready, m, 2 * i - 4))
                act.copy(b_all[:, i % 3, :], src[:, :]).then_inc(b_ready.sem, 1)

            def exponentials(m, i):
                for s in (2 * i, 2 * i + 1):
                    j, n = channel_tile(s), i % NST
                    if s >= 4:
                        act.wait_ge(scanned.sem, at(scanned, m, s - 3))
                    act.activation(decay[:, s % 4, :], dt[:, j, :], ACT.Exp,
                                   scale=neg_a[:, j * NST + n:j * NST + n + 1]).then_inc(decay_ready.sem, 1)

            def run(units, m, r):
                mf, rf = [0], [0]

                def from_m():
                    mf[0] += 1
                    act.wait_ge(m_full.sem, at(m_full, m, mf[0]))
                    return ps_m

                def from_r():
                    rf[0] += 1
                    act.wait_ge(r_full.sem, at(r_full, r, rf[0]))
                    return ps_r[(rf[0] - 1) % 2]

                for unit, i in units:
                    if unit == "m_norm":
                        for k in range(KC):
                            src = from_m()
                            act.copy(xnT[:, k, :], src[:, :]).then_inc(n_turned["m"].sem, 1)
                    elif unit == "m_in":
                        src = from_m()
                        if i < JD:
                            act.copy(xs[:, i, TAPS - 1:], src[:, :]).then_inc(xs_ready.sem, 1)
                        else:
                            act.activation(sz[:, i - JD, :], src[:, :], ACT.Silu).then_inc(sz_ready.sem, 1)
                    elif unit == "m_xproj":
                        for j in range(JD):
                            act.wait_ge(conv_tap.sem, at(conv_tap, m, JD * (TAPS - 1) + j + 1))
                            act.activation(xc[:, j, :], xc[:, j, :], ACT.Silu).then_inc(xc_ready.sem, 1)
                        src = from_m()
                        act.copy(dtr[:, :], src[0:RANK, :]).then_inc(dtr_ready.sem, 1)
                        src = from_m()
                        act.copy(bcf[:, :], src[0:6 * NST, :]).then_inc(bcf_ready.sem, 1)
                    elif unit == "m_dt":
                        if i == 0:
                            act.preload_act_table_set("natural_log_exp_and_others")
                        src, bias = from_m(), col("b_dt", i)
                        act.activation(dtx[:, i, :], src[:, :], ACT.Abs, bias=bias).then_inc(sp_abs.sem, 1)
                        act.activation(dt[:, i, :], src[:, :], ACT.Relu, bias=bias).then_inc(sp_relu.sem, 1)
                        act.wait_ge(sp_abs.sem, at(sp_abs, m, i + 1))
                        act.activation(dtx[:, i, :], dtx[:, i, :], ACT.Exp, scale=-1.0).then_inc(sp_exp.sem, 1)
                        act.wait_ge(sp_rest.sem, at(sp_rest, m, i + 1))
                        act.activation(u1[:, i % 2, :], u1[:, i % 2, :], ACT.Ln).then_inc(sp_ln.sem, 1)
                    elif unit == "m_step":
                        if i == 0:
                            copy_b(m, 0, from_m())
                            copy_b(m, 1, from_m())
                            act.wait_ge(dt_ready.sem, at(dt_ready, m, JD))
                            exponentials(m, 0)
                        if i + 2 < STEPS:
                            copy_b(m, i + 2, from_m())
                        if i + 1 < STEPS:
                            exponentials(m, i + 1)
                    elif unit == "r_norm":
                        for k in range(KC):
                            src = from_r()
                            act.copy(xT[:, k, 1:T + 1], src[:, :]).then_inc(n_turned["r"].sem, 1)
                    elif unit == "r_up":
                        src = from_r()
                        if i % FM >= 2:
                            act.wait_ge(v_read.sem, at(v_read, r, i - 1 + (4 if i >= FM else 0)))
                        if i < FM:
                            act.activation(sg[:, i % 2, :], src[:, :], ACT.Silu).then_inc(sg_ready.sem, 1)
                        else:
                            act.activation(sg[:, i % 2, :], src[:, :], ACT.Tanh, scale=0.5).then_inc(sg_ready.sem, 1)
                    elif unit == "r_recept":
                        src = from_r()
                        act.activation(yr[:, i, :], src[:, :], ACT.Tanh, bias=half_br[:, i:i + 1], scale=0.5)\
                            .then_inc(recept_ready.sem, 1)
                    elif unit == "r_kv":
                        if i == 0:
                            act.preload_act_table_set("natural_log_exp_and_others")
                        src = from_r()
                        if i:
                            act.wait_ge(e_summed.sem, at(e_summed, r, i))
                            act.wait_ge(den_ready.sem, at(den_ready, r, i))
                        else:
                            act.wait_ge(out_stored.sem, at(out_stored, r, 0))
                        act.activation(ek, src[:, :], ACT.Identity, bias=col("bk", i)).then_inc(kb_ready.sem, 1)
                        act.activation(eu, src[:, :], ACT.Exp, bias=ubk[:, i:i + 1]).then_inc(eu_ready.sem, 1)
                        src = from_r()
                        act.activation(vv, src[:, :], ACT.Identity, bias=col("bv", i)).then_inc(vv_ready.sem, 1)
                        if i:
                            reciprocal(r, i - 1)
                        act.wait_ge(k_clipped.sem, at(k_clipped, r, i + 1))
                        act.activation(ek, ek, ACT.Exp).then_inc(e_ready.sem, 1)
                    elif unit == "r_kvlast":
                        reciprocal(r, CT - 1)

            sequences(act, run)

        @block.vector
        def _(dve):
            dve.wait_ge(par_in.sem, 32)
            d0, k0, q0 = PC["decay"], PC["bk"], PC["U"]
            dve.tensor_scalar(neg_w[:, :], par[:, d0:d0 + CT], 0.0, -1.0, ALU.max, ALU.mult)\
                .then_inc(setup_dve.sem, 1)
            dve.tensor_tensor(ubk[:, :], par[:, q0:q0 + CT], par[:, k0:k0 + CT], ALU.add).then_inc(setup_dve.sem, 1)
            r0 = PC["br"]
            dve.tensor_scalar(half_br[:, :], par[:, r0:r0 + CT], 0.5, None, ALU.mult).then_inc(setup_dve.sem, 1)
            dve.wait_ge(setup_act.sem, 1)
            dve.tensor_scalar(neg_a[:, :], neg_a[:, :], -1.0, None, ALU.mult).then_inc(setup_dve.sem, 1)
            dve.wait_ge(ffn_in.sem, 64)
            for w in (wgate, wup, wdown):
                dve.tensor_scalar(w[:, :, :], w[:, :, :].bitcast(i32), float(np.float32(1.0 / 127.0)), None, ALU.mult)\
                    .then_inc(setup_dve.sem, 1)
            dve.wait_ge(pool_const.sem, 7)

            def norm(f, seq, i, src, dst):
                for t in range(TT):
                    dve.bn_stats(stats[f][:, t, :], src[:, t, :]).then_inc(n_stats[f].sem, 1)
                for t in range(TT):
                    dve.wait_ge(n_stats[f].sem, at(n_stats[f], seq, TT * i + t + 1))
                    dve.sem_inc(carried.sem, 1)
                    dve.bn_aggr(moments[f][:, t, :], stats[f][:, t, :]).then_inc(n_moments[f].sem, 1)
                dve.wait_ge(n_moments[f].sem, at(n_moments[f], seq, TT * (i + 1)))
                dve.tensor_scalar(var_eps[f][:, :], moments[f][:, :, 1], EPS_LN, None, ALU.add)\
                    .then_inc(n_var[f].sem, 1)
                dve.wait_ge(n_rstd[f].sem, at(n_rstd[f], seq, i + 1))
                for t in range(TT):
                    last = dve.tensor_scalar(dst[:, t, :], src[:, t, :], moments[f][:, t, 0:1], rstd[f][:, t:t + 1],
                                             ALU.subtract, ALU.mult)
                last.then_inc(n_normed[f].sem, 1)

            def times_c(m, s):
                dve.wait_ge(scanned.sem, at(scanned, m, s + 1))
                dve.wait_ge(c_full.sem, at(c_full, m, s // 2 + 1))
                if s >= 4:
                    dve.wait_ge(y_added.sem, at(y_added, m, s - 3))
                dve.tensor_tensor(hc[:, s % 4, :], h[:, s % 3, :], ps_c[s // 2 % 2][:, :], ALU.mult)\
                    .then_inc(hc_ready.sem, 1)

            def weighted(r, c):
                dve.wait_ge(rec_ready.sem, at(rec_ready, r, c + 1))
                dve.tensor_tensor(den[:, :], den[:, :], rec[:, :], ALU.mult).then_inc(newton.sem, 1)
                dve.wait_ge(newton.sem, at(newton, r, 3 * c + 1))
                dve.scalar_tensor_tensor(den[:, :], den[:, :], 2.0, rec[:, :], ALU.subtract, ALU.mult)\
                    .then_inc(newton.sem, 1)
                dve.wait_ge(num_ready.sem, at(num_ready, r, c + 1))
                dve.wait_ge(newton.sem, at(newton, r, 3 * c + 2))
                dve.scalar_tensor_tensor(num[:, :], den[:, :], -0.5, num[:, :], ALU.mult, ALU.mult)\
                    .then_inc(newton.sem, 1)
                dve.wait_ge(recept_ready.sem, at(recept_ready, r, c + 1))
                dve.wait_ge(newton.sem, at(newton, r, 3 * c + 3))
                dve.scalar_tensor_tensor(yr[:, c, :], yr[:, c, :], 1.0, num[:, :], ALU.add, ALU.mult)\
                    .then_inc(wkv_ready.sem, 1)

            def run(units, m, r):
                vf = [0]

                def from_v():
                    vf[0] += 1
                    dve.wait_ge(v_full.sem, at(v_full, r, vf[0]))

                def add_residual(half, dst):
                    from_v()
                    dve.tensor_tensor(dst[:, 2 * half:2 * half + 2, :].rearrange("p t c -> p (t c)"), ps_v[:, :],
                                      xr[:, 2 * half:2 * half + 2, :].rearrange("p t c -> p (t c)"), ALU.add)\
                        .then_inc(v_read.sem, 1)

                for unit, i in units:
                    if unit == "m_norm":
                        dve.wait_ge(x_loaded.sem, at(x_loaded, m, 16))
                        norm("m", m, 0, xin, xin)
                    elif unit == "m_conv":
                        for j in range(JD):
                            if i == 0:
                                dve.wait_ge(xs_ready.sem, at(xs_ready, m, j + 1))
                                dve.tensor_scalar(xc[:, j, :], xs[:, j, 0:T], col("conv_w", TAPS * j), col("conv_b", j),
                                                  ALU.mult, ALU.add).then_inc(conv_tap.sem, 1)
                            else:
                                dve.wait_ge(conv_tap.sem, at(conv_tap, m, JD * (i - 1) + j + 1))
                                dve.scalar_tensor_tensor(xc[:, j, :], xs[:, j, i:i + T], col("conv_w", TAPS * j + i),
                                                         xc[:, j, :], ALU.mult, ALU.add).then_inc(conv_tap.sem, 1)
                    elif unit == "m_xproj":
                        n2, n4, n6 = 2 * NST, 4 * NST, 6 * NST
                        dve.wait_ge(bcf_ready.sem, at(bcf_ready, m, 1))
                        dve.tensor_copy(bc3[:, :], bcf[:, :]).then_inc(bc_split.sem, 1)
                        dve.wait_ge(bc_split.sem, at(bc_split, m, 1))
                        dve.tensor_tensor(bcf[:, :], bcf[:, :], bc3[:, :], ALU.subtract).then_inc(bc_split.sem, 1)
                        dve.wait_ge(bc_split.sem, at(bc_split, m, 2))
                        dve.tensor_copy(bc3[n2:n4, :], bcf[n2:n4, :]).then_inc(bc_split.sem, 1)
                        dve.tensor_copy(bc3[n4:n6, :], bcf[n4:n6, :]).then_inc(bc_split.sem, 1)
                        dve.wait_ge(bc_split.sem, at(bc_split, m, 4))
                        dve.tensor_tensor(bc3[n4:n6, :], bcf[n4:n6, :], bc3[n4:n6, :], ALU.subtract)\
                            .then_inc(bc_split.sem, 1)
                    elif unit == "m_dt":
                        u = u1[:, i % 2, :]
                        if i == 0:
                            dve.wait_ge(bc_split.sem, at(bc_split, m, 5))
                        dve.wait_ge(sp_exp.sem, at(sp_exp, m, i + 1))
                        dve.tensor_scalar(u, dtx[:, i, :], 1.0, None, ALU.add).then_inc(sp_u.sem, 1)
                        dve.wait_ge(sp_u.sem, at(sp_u, m, i + 1))
                        dve.scalar_tensor_tensor(dtx[:, i, :], u, 1.0, dtx[:, i, :], ALU.subtract, ALU.subtract)\
                            .then_inc(sp_rest.sem, 1)
                        dve.wait_ge(sp_rest.sem, at(sp_rest, m, i + 1))
                        dve.wait_ge(sp_ln.sem, at(sp_ln, m, i + 1))
                        dve.tensor_tensor(u, u, dtx[:, i, :], ALU.subtract).then_inc(sp_sum.sem, 1)
                        dve.wait_ge(sp_sum.sem, at(sp_sum, m, i + 1))
                        dve.wait_ge(sp_relu.sem, at(sp_relu, m, i + 1))
                        dve.tensor_tensor(dt[:, i, :], dt[:, i, :], u, ALU.add).then_inc(dt_ready.sem, 1)
                    elif unit == "m_step":
                        for s in (2 * i, 2 * i + 1):
                            dve.wait_ge(decay_ready.sem, at(decay_ready, m, s + 1))
                            dve.wait_ge(bu_ready.sem, at(bu_ready, m, s + 1))
                            if s >= 3:
                                dve.wait_ge(hc_ready.sem, at(hc_ready, m, s - 2))
                            dve.tensor_tensor_scan(h[:, s % 3, :], decay[:, s % 4, :], bu[:, s % 2, :], 0.0,
                                                   ALU.mult, ALU.add).then_inc(scanned.sem, 1)
                            if s % (2 * NST):
                                times_c(m, s - 1)
                    elif unit == "m_gate":
                        times_c(m, 2 * NST * (i + 1) - 1)
                        for j in (2 * i, 2 * i + 1):
                            dve.wait_ge(y_added.sem, at(y_added, m, 2 * NST * (i + 1) - 1 + j % 2))
                            dve.scalar_tensor_tensor(dtx[:, j, :], xc[:, j, :], col("D", j), ps_y[j % 2][:, :],
                                                     ALU.mult, ALU.add).then_inc(y_read.sem, 1)
                        for j in (2 * i, 2 * i + 1):
                            dve.wait_ge(sz_ready.sem, at(sz_ready, m, j + 1))
                            dve.wait_ge(y_read.sem, at(y_read, m, j + 1))
                            dve.tensor_tensor(dtx[:, j, :], dtx[:, j, :], sz[:, j, :], ALU.mult)\
                                .then_inc(gated.sem, 1)
                    elif unit == "m_post":
                        dve.wait_ge(x_loaded.sem, at(x_loaded, m, 32))
                        for half in range(2):
                            part = slice(2 * half, 2 * half + 2)
                            dve.wait_ge(c_full.sem, at(c_full, m, STEPS + half + 1))
                            dve.tensor_tensor(xr[:, part, :].rearrange("p t c -> p (t c)"), ps_c[half][:, :],
                                              xin[:, part, :].rearrange("p t c -> p (t c)"), ALU.add)\
                                .then_inc(m_done.sem, 1)
                    elif unit == "r_norm":
                        if i == 0:
                            dve.wait_ge(m_done.sem, at(m_done, r, 2))
                        else:
                            dve.wait_ge(v_read.sem, at(v_read, r, vf[0]))
                        norm("r", r, i, xr, xnr)
                    elif unit == "r_up":
                        dve.wait_ge(sg_ready.sem, at(sg_ready, r, i + 1))
                        if i < FM:
                            from_v()
                            dve.tensor_tensor(hf[:, i, :], ps_v[:, :], sg[:, i % 2, :], ALU.mult)\
                                .then_inc(v_read.sem, 1)
                        else:
                            gate = ps_r[GATE_BANK[i] % 2]
                            dve.scalar_tensor_tensor(sg[:, i % 2, :], sg[:, i % 2, :], 1.0, gate[:, :],
                                                     ALU.add, ALU.mult).then_inc(gate_read.sem, 1)
                            dve.wait_ge(gate_read.sem, at(gate_read, r, i - FM + 1))
                            from_v()
                            dve.scalar_tensor_tensor(hf[:, i - FM, :], sg[:, i % 2, :], 0.5, ps_v[:, :],
                                                     ALU.mult, ALU.mult).then_inc(v_read.sem, 1)
                    elif unit == "r_down":
                        add_residual(i % 2, xr if i < 2 else xout)
                    elif unit == "r_wo":
                        add_residual(i, xr)
                    elif unit == "r_mix":
                        for q in range(3):
                            for k in range(KC):
                                dve.wait_ge(mix_scaled.sem, at(mix_scaled, r, KC * q + k + 1))
                                dve.scalar_tensor_tensor(mix[:, q, k, :], xT[:, k, 2:T + 2], 1.0 - MIX[q],
                                                         mix[:, q, k, :], ALU.mult, ALU.add)\
                                    .then_inc(mix_ready.sem, 1)
                    elif unit == "r_kv":
                        dve.wait_ge(kb_ready.sem, at(kb_ready, r, i + 1))
                        dve.scalar_tensor_tensor(ek, t_left[:, :], neg_w[:, i:i + 1], ek, ALU.mult, ALU.add)\
                            .then_inc(k_decayed.sem, 1)
                        dve.wait_ge(k_decayed.sem, at(k_decayed, r, i + 1))
                        dve.tensor_scalar(ek, ek, LO, HI, ALU.max, ALU.min).then_inc(k_clipped.sem, 1)
                        if i:
                            weighted(r, i - 1)
                        dve.wait_ge(e_ready.sem, at(e_ready, r, i + 1))
                        if i:
                            dve.wait_ge(den_ready.sem, at(den_ready, r, i))
                        dve.tensor_tensor_scan(sums[:, 0, 1:], ones[:, 0:1].to_broadcast([P, T]), ek, 0.0, ALU.mult, ALU.add)\
                            .then_inc(e_summed.sem, 1)
                        dve.wait_ge(ev_ready.sem, at(ev_ready, r, i + 1))
                        dve.tensor_tensor_scan(sums[:, 1, 1:], ones[:, 0:1].to_broadcast([P, T]), ev, 0.0, ALU.mult, ALU.add)\
                            .then_inc(ev_summed.sem, 1)
                        dve.wait_ge(ev_summed.sem, at(ev_summed, r, i + 1))
                        dve.wait_ge(euv_ready.sem, at(euv_ready, r, i + 1))
                        dve.tensor_tensor(num[:, :], sums[:, 1, 0:T], num[:, :], ALU.add).then_inc(num_ready.sem, 1)
                    elif unit == "r_kvlast":
                        weighted(r, CT - 1)

            sequences(dve, run)

        @block.tensor
        def _(pe):
            pe.wait_ge(par_in.sem, 32)
            pe.wait_ge(weights_in.sem, 12 * 16)
            pe.wait_ge(pool_const.sem, 10)
            pe.wait_ge(setup_dve.sem, 7)

            def turn(src, k, dst, full):
                for t in range(TT):
                    last = pe.transpose(dst[:, P * t:P * (t + 1)], src[:, t, P * k:P * (k + 1)], ident[:, :])
                last.then_inc(full.sem, 1)

            def project(dst, pairs, full):
                for n, (lhs, rhs) in enumerate(pairs):
                    last = pe.matmul(dst, lhs, rhs, start=n == 0, stop=n == len(pairs) - 1)
                last.then_inc(full.sem, 1)

            def to_tokens(dst, half, acts, weights, tiles, full, bias):
                for t in (2 * half, 2 * half + 1):
                    d = dst[:, C * (t % 2):C * (t % 2 + 1)]
                    if bias:
                        pe.matmul(d, ones[0:1, 0:P], bo[:, :], start=True, stop=False)
                    for k in range(tiles):
                        last = pe.matmul(d, acts[:, k, P * t:P * (t + 1)], weights[:, k, :],
                                         start=k == 0 and not bias, stop=k == tiles - 1)
                last.then_inc(full.sem, 1)

            def run(units, m, r):
                m_freed, r_freed, v_uses = [], [], [0]

                def to_m(freed, count):
                    if m_freed:
                        pe.wait_ge(m_freed[-1][0].sem, at(m_freed[-1][0], m, m_freed[-1][1]))
                    m_freed.append((freed, count))
                    return ps_m

                def to_r(freed, count):
                    if len(r_freed) >= 2:
                        pe.wait_ge(r_freed[-2][0].sem, at(r_freed[-2][0], r, r_freed[-2][1]))
                    r_freed.append((freed, count))
                    return ps_r[(len(r_freed) - 1) % 2]

                def to_v():
                    if v_uses[0]:
                        pe.wait_ge(v_read.sem, at(v_read, r, v_uses[0]))
                    v_uses[0] += 1
                    return ps_v

                def spread_b(i):
                    n = i % NST
                    pe.matmul(to_m(b_ready, i + 1)[:, :], select[:, n, :], bc3[:, :], start=True, stop=True)\
                        .then_inc(m_full.sem, 1)

                def spread_c(i):
                    n = i % NST
                    if i >= 2:
                        pe.wait_ge(hc_ready.sem, at(hc_ready, m, 2 * i - 2))
                    pe.matmul(ps_c[i % 2][:, :], select[:, NST + n, :], bc3[:, :], start=True, stop=True)\
                        .then_inc(c_full.sem, 1)

                def add_y(s):
                    n = s // 2 % NST
                    if n == 0 and s >= 2 * NST:
                        pe.wait_ge(y_read.sem, at(y_read, m, channel_tile(s) - 1))
                    pe.wait_ge(hc_ready.sem, at(hc_ready, m, s + 1))
                    pe.matmul(ps_y[s % 2][:, :], ident[:, :], hc[:, s % 4, :], start=n == 0, stop=n == NST - 1)\
                        .then_inc(y_added.sem, 1)

                for unit, i in units:
                    if unit == "m_norm":
                        pe.wait_ge(n_normed["m"].sem, at(n_normed["m"], m, 1))
                        for k in range(KC):
                            turn(xin, k, to_m(n_turned["m"], k + 1), m_full)
                    elif unit == "m_in":
                        if i == 0:
                            pe.wait_ge(n_turned["m"].sem, at(n_turned["m"], m, KC))
                        dst = to_m(xs_ready, i + 1) if i < JD else to_m(sz_ready, i - JD + 1)
                        project(dst[:, :], [(win[:, k, P * i:P * (i + 1)], xnT[:, k, :]) for k in range(KC)], m_full)
                    elif unit == "m_xproj":
                        pe.wait_ge(xc_ready.sem, at(xc_ready, m, JD))
                        project(to_m(dtr_ready, 1)[0:RANK, :],
                                [(wx_dt[:, j, :], xc[:, j, :]) for j in range(JD)], m_full)
                        project(to_m(bcf_ready, 1)[0:6 * NST, :],
                                [(wx_bc[:, j, :, :].rearrange("p a b -> p (a b)"), xc[:, j, :]) for j in range(JD)],
                                m_full)
                    elif unit == "m_dt":
                        if i == 0:
                            pe.wait_ge(dtr_ready.sem, at(dtr_ready, m, 1))
                        project(to_m(sp_relu, i + 1)[:, :], [(wdt[:, P * i:P * (i + 1)], dtr[:, :])], m_full)
                    elif unit == "m_step":
                        if i == 0:
                            pe.wait_ge(bc_split.sem, at(bc_split, m, 5))
                            spread_b(0)
                            spread_b(1)
                            spread_c(0)
                        if i + 2 < STEPS:
                            spread_b(i + 2)
                        if i + 1 < STEPS:
                            spread_c(i + 1)
                        if i % NST:
                            add_y(2 * i - 2)
                            add_y(2 * i - 1)
                    elif unit == "m_gate":
                        add_y(2 * NST * (i + 1) - 2)
                        add_y(2 * NST * (i + 1) - 1)
                    elif unit == "m_post":
                        pe.wait_ge(gated.sem, at(gated, m, JD))
                        for half in range(2):
                            to_tokens(ps_c[half], half, dtx, wout, JD, c_full, False)
                    elif unit == "r_norm":
                        pe.wait_ge(n_normed["r"].sem, at(n_normed["r"], r, i + 1))
                        for k in range(KC):
                            turn(xnr, k, to_r(n_turned["r"], KC * i + k + 1), r_full)
                    elif unit == "r_up":
                        if i % FM == 0:
                            pe.wait_ge(n_turned["r"].sem, at(n_turned["r"], r, KC if i == 0 else 3 * KC))
                        f = i % FM
                        project((to_r(sg_ready, i + 1) if i < FM else to_r(gate_read, i - FM + 1))[:, :],
                                [(wgate[:, k, P * f:P * (f + 1)], xT[:, k, 1:T + 1]) for k in range(KC)], r_full)
                        project(to_v()[:, :],
                                [(wup[:, k, P * f:P * (f + 1)], xT[:, k, 1:T + 1]) for k in range(KC)], v_full)
                    elif unit == "r_down":
                        to_tokens(to_v(), i % 2, hf, wdown, FM, v_full, False)
                    elif unit == "r_recept":
                        if i == 0:
                            pe.wait_ge(mix_ready.sem, at(mix_ready, r, KC))
                        project(to_r(recept_ready, i + 1)[:, :],
                                [(wr[:, k, P * i:P * (i + 1)], mix[:, 0, k, :]) for k in range(KC)], r_full)
                    elif unit == "r_kv":
                        if i == 0:
                            pe.wait_ge(mix_ready.sem, at(mix_ready, r, 3 * KC))
                        project(to_r(eu_ready, i + 1)[:, :],
                                [(wk[:, k, P * i:P * (i + 1)], mix[:, 1, k, :]) for k in range(KC)], r_full)
                        project(to_r(vv_ready, i + 1)[:, :],
                                [(wv[:, k, P * i:P * (i + 1)], mix[:, 2, k, :]) for k in range(KC)], r_full)
                    elif unit == "r_wo":
                        if i == 0:
                            pe.wait_ge(wkv_ready.sem, at(wkv_ready, r, CT))
                        to_tokens(to_v(), i, yr, wo, CT, v_full, True)

            sequences(pe, run)


def kernel(**inputs):
    import concourse.bacc as bacc
    from concourse.bass_utils import run_bass_kernel_spmd

    a = {k.replace("L0_attn_", "").replace("L0_", ""): np.asarray(v) for k, v in inputs.items()}

    def tiles(v, n):
        return v.reshape(n, P, -1).transpose(1, 0, 2).reshape(P, -1)

    params = np.concatenate([tiles(a["a_conv_w"], JD), tiles(a["a_conv_b"], JD), tiles(a["a_b_dt"], JD),
                             tiles(a["a_A_log"], JD), tiles(a["a_D_param"], JD), tiles(a["b_br"], CT),
                             tiles(a["b_bk"], CT), tiles(a["b_bv"], CT), tiles(a["b_time_decay"], CT),
                             tiles(a["b_U"], CT)], axis=1)
    arrays = {"x": a["a_x"], "w_in": a["a_W_in"].T, "w_x": a["a_W_x"].T, "w_dt": a["a_W_dt"].T,
              "w_out": a["a_W_out"].T, "w_gate": a["ffn_w_gate"].T, "w_up": a["ffn_w_up"].T,
              "w_down": a["ffn_w_down"].T, "w_r": a["b_Wr"].T, "w_k": a["b_Wk"].T, "w_v": a["b_Wv"].T,
              "w_o": a["b_Wo"].T, "b_o": a["b_bo"].reshape(1, C), "params": params,
              "ident": np.eye(P, dtype=np.float32),
              "steps_left": np.arange(T - 1, -1, -1, dtype=np.float32).reshape(1, T)}
    arrays = {k: np.ascontiguousarray(v) for k, v in arrays.items()}
    nc = bacc.Bacc("TRN2", target_bir_lowering=False, num_devices=1)
    args = [nc.dram_tensor(f"{k}_dram", v.shape, mybir.dt.from_np(v.dtype), kind="ExternalInput").ap()
            for k, v in arrays.items()]
    out = nc.dram_tensor("out_dram", (NSEQ, T, C), mybir.dt.float32, kind="ExternalOutput").ap()
    hybrid_block(nc, *args, out)
    r = run_bass_kernel_spmd(nc, [{f"{k}_dram": v for k, v in arrays.items()}], core_ids=[0])
    return r.results[0]["out_dram"]
```

```python
import numpy as np
import concourse.bass as bass
from concourse import mybir
from contextlib import ExitStack

NSEQ, T, C = 8, 512, 256
DIN, NST, TAPS, RANK = 512, 16, 4, 64
HID = 768
ATT = 1024
P = 128
KC, JD, FM, CT, TT = C // P, DIN // P, HID // P, ATT // P, T // P
EPS_LN = 1e-5
EPS = float(np.exp(-1 / 12))
MIX = (EPS / 2.0, EPS + 0.3 / 11, EPS)
LO, HI = -20.0, 10.0
PC = {}
_at = 0
for _n, _w in (("conv_w", JD * TAPS), ("conv_b", JD), ("b_dt", JD), ("A_log", JD * NST), ("D", JD),
               ("br", CT), ("bk", CT), ("bv", CT), ("decay", CT), ("U", CT)):
    PC[_n] = _at
    _at += _w
NPAR = _at

STEPS = JD // 2 * NST


def in_time(*timed):
    return sorted((x for part in timed for x in part), key=lambda x: x[0])


def norm(f, i, at=0.0):
    return [(at, f + "v_stats", i), (at + 2, "g_rstd_" + f, i), (at + 3, f + "v_norm", i),
            (at + 5, f + "p_turn", i), (at + 6.5, f + "a_turn", i)]


def after(units, gap, *then):
    for more in then:
        start = max(x[0] for x in units) + gap
        units = units + [(start + t, u, i) for t, u, i in more]
    return units


def ffn(first, half):
    units = []
    for m in range(FM):
        t = 3.4 * m
        units += [(t, "p_gate", first + m), (t + 3, "a_gate", first + m), (t + 3.3, "p_up", first + m),
                  (t + 5, "v_up", first + m)]
    t = 3.4 * FM + 3
    return units + [(t, "p_down", half), (t + 2, "p_down", half + 1), (t + 4.5, "v_down", half),
                    (t + 7.5, "v_down", half + 1)]


M_HEAD = after(norm("m", 0), 1.5, [x for m in range(2 * JD) for x in ((2.5 * m, "p_in", m), (2.5 * m + 1.8, "a_in", m))]
               + [(2.5 * JD + 1.5 + 2.6 * k, "v_conv", k) for k in range(TAPS)],
               [(0, "a_xc", 0), (2, "p_xproj", 0), (4, "a_xproj", 0), (5, "p_xproj", 1), (8, "a_xproj", 1),
                (9, "v_split", 0)])
M_DT = [x for j in range(JD) for x in
        ((3.0 * j, "p_dt", j), (3.0 * j + 1, "a_dt", j), (3.0 * j + 2.5, "v_dt", j), (3.0 * j + 3.6, "a_ln", j),
         (3.0 * j + 4.2, "v_dtsum", j), (3.0 * j + 5.5, "g_dtx", j))]
M_SCAN = []
for _i in range(STEPS):
    M_SCAN += [(_i, "m_step", _i)]
    if _i % NST == NST - 1:
        M_SCAN += [(_i + 0.5, "m_gate", _i // NST)]
M_POST = [(0, "m_post", 0)]

MIXING = after(norm("r", 1), 1, [x for q in range(3) for x in ((1.2 * q, "g_mix", q), (1.2 * q + 1.5, "v_mix", q))])
RECEPT = [x for c in range(CT) for x in ((1.8 * c, "p_recept", c), (1.8 * c + 2.5, "a_recept", c))]
KV = [(4.4 * (c + t), u, c) for c in range(CT) for t, u in
      ((0, "p_k"), (0.25, "p_v"), (0.5, "a_kv"), (0.75, "v_exp"), (0.78, "g_eu"), (1, "a_e"), (1.25, "g_ev"),
       (1.3, "v_esum"), (1.6, "g_den"), (1.75, "v_evsum"), (2, "a_rec"), (2.25, "v_wkv"))]
WO = [(0, "p_wo", 0), (3.4, "p_wo", 1), (4.5, "v_wo", 0), (7, "v_wo", 1)]
FFN1 = after(norm("r", 0), 0.5, ffn(0, 0))
LATE = after(after(RECEPT, -1.5, KV), 0.5, WO, norm("r", 2), ffn(FM, 2))


def merged(a, b):
    parts = []
    for units in (a, b):
        whole = max([x[0] for x in units] + [0]) + 1
        parts.append([(t / whole, u, i) for t, u, i in units])
    return [(u, i) for _, u, i in in_time(*parts)]


MAMBA = merged(M_HEAD, []) + merged(M_DT, []) + merged(M_SCAN, []) + merged(M_POST, [])
REST = merged(FFN1, []) + merged(MIXING, []) + merged(LATE, [])
BOTH = merged(FFN1, M_HEAD) + merged(MIXING, M_DT) + merged(LATE, M_SCAN) + merged(M_POST, [])

R_UNITS = ("rp_turn", "p_gate", "p_recept", "p_k", "p_v", "p_down", "p_wo")
R_BANK, R_ORDER = {}, []
for _u, _i in REST:
    if _u in R_UNITS and not (_u in ("p_down", "p_wo") and _i % 2 == 0):
        for _k in range(KC if _u == "rp_turn" else 1):
            R_BANK[_u, _i, _k] = len(R_ORDER) % 2
            R_ORDER.append((_u, _i, _k))


V_COUNT = {}
for _u, _i in REST:
    if _u in ("v_up", "v_down", "v_wo"):
        V_COUNT[_u, _i] = len(V_COUNT) + 1
V_USES = [k for k in V_COUNT if k[0] == "v_up" or k[1] % 2 == 0]


class Signal:

    def __init__(self, sem, per, first=0):
        self.sem, self.per, self.first = sem, per, first


def at(signal, seq, count):
    return seq * signal.per + (signal.first + count)


def hybrid_block(nc, x, w_in, w_x, w_dt, w_out, w_gate, w_up, w_down, w_r, w_k, w_v, w_o, b_o, params,
                 ident_in, steps_left, out):
    f32, bf16, i32 = mybir.dt.float32, mybir.dt.bfloat16, mybir.dt.int32
    ALU, ACT = mybir.AluOpType, mybir.ActivationFunctionType
    x_v = x.rearrange("s (t p) c -> s p t c", p=P)
    out_v = out.rearrange("s (t p) c -> s p t c", p=P)

    with ExitStack() as ctx:
        def sb(name, shape, dt=f32):
            return ctx.enter_context(nc.sbuf_tensor(name, shape, dt))

        def bank(name):
            return ctx.enter_context(nc.psum_tensor(name, [P, T], f32))

        def signal(name, per, first=0):
            return Signal(ctx.enter_context(nc.semaphore(name)), per, first)

        win = sb("win", [P, KC, 2 * DIN])
        wx_dt = sb("wx_dt", [P, JD, RANK])
        wx_bc = sb("wx_bc", [P, JD, 3, 2 * NST])
        wdt = sb("wdt", [RANK, DIN])
        wout = sb("wout", [P, JD, C])
        wgate = sb("wgate", [P, KC, HID])
        wup = sb("wup", [P, KC, HID])
        wdown = sb("wdown", [P, FM, C])
        wr, wk, wv = (sb(n, [P, KC, ATT]) for n in ("wr", "wk", "wv"))
        wo = sb("wo", [P, CT, C])
        bo = sb("bo", [1, C])
        par = sb("par", [P, NPAR])
        neg_a = sb("neg_a", [P, JD * NST])
        neg_w = sb("neg_w", [P, CT])
        ubk = sb("ubk", [P, CT])
        half_br = sb("half_br", [P, CT])
        ident = sb("ident", [P, P])
        select = sb("select", [3 * 2 * NST, 2 * NST, P], bf16)
        t_left = sb("t_left", [P, T])
        ones = sb("ones", [P, P])
        minus_half = sb("minus_half", [P, TT])

        xin = sb("xin", [P, TT, C])
        xs = sb("xs", [P, JD, T + TAPS - 1])
        xc = sb("xc", [P, JD, T])
        sz = sb("sz", [P, JD, T])
        dtx = sb("dtx", [P, JD, T])
        u1 = sb("u1", [P, 1, T])
        bcf = u1[0:3 * 2 * NST, 0, :]
        bc3 = sb("bc3", [3 * 2 * NST, T], bf16)
        b_all = sb("b_all", [P, 3, T])
        decay = sb("decay", [P, 4, T])
        xnT = decay[:, 0:KC, :]
        dtr = b_all[0:RANK, 0, :]
        bu = sb("bu", [P, 2, T])
        h = sb("h", [P, 3, T])
        hc = sb("hc", [P, 4, T])
        dt = xs[:, :, TAPS - 1:]

        xr = sb("xr", [P, TT, C])
        xT = sb("xT", [P, KC, T + 2])
        mix = sb("mix", [P, 3, KC, T])
        hf = mix[:, :, :, :].rearrange("p a k t -> p (a k) t")
        yr = sb("yr", [P, CT, T])
        kv = sb("kv", [P, 4, T])
        ek = [kv[:, 0, :], mix[:, 0, 0, :]]
        vv = [kv[:, 1, :], mix[:, 0, 1, :]]
        ev = kv[:, 2, :]
        xnr = kv[:, 0:2, :].rearrange("p a (t c) -> p (a t) c", c=C)
        xout = kv[:, 2:4, :].rearrange("p a (t c) -> p (a t) c", c=C)
        sums = sb("sums", [P, 2, T + 1])
        sg = sums[:, :, 1:]
        num = [sb(n, [P, T])[:, :] for n in ("num0", "num1")]
        den = [sb("den0", [P, T])[:, :], kv[:, 3, :]]
        rec = sb("rec", [P, T])

        stats = {f: sb(f + "_stats", [P, TT, 6]) for f in "mr"}
        moments = {f: sb(f + "_moments", [P, TT, 2]) for f in "mr"}
        var_eps = {f: sb(f + "_var_eps", [P, TT]) for f in "mr"}
        rstd = {f: sb(f + "_rstd", [P, TT]) for f in "mr"}

        ps_m = bank("ps_m")
        ps_c = [bank(f"ps_c{i}") for i in range(2)]
        ps_y = [bank(f"ps_y{i}") for i in range(2)]
        ps_r = [bank(f"ps_r{i}") for i in range(2)]
        ps_v = bank("ps_v")

        weights_in = signal("weights_in", 0)
        par_in = signal("par_in", 0)
        ffn_in = signal("ffn_in", 0)
        pool_const = signal("pool_const", 0)
        setup_act = signal("setup_act", 0)
        setup_dve = signal("setup_dve", 0)
        carried = signal("carried", 0)
        x_loaded = signal("x_loaded", 32)
        out_stored = signal("out_stored", 16, first=16)
        n_stats = {"m": signal("m_stat", TT), "r": signal("r_stat", 3 * TT)}
        n_moments = {"m": signal("m_mom", TT), "r": signal("r_mom", 3 * TT)}
        n_var = {"m": signal("m_var", 1), "r": signal("r_var", 3)}
        n_rstd = {"m": signal("m_rstd_done", 1), "r": signal("r_rstd_done", 3)}
        n_normed = {"m": signal("m_normed", 1), "r": signal("r_normed", 3)}
        n_turned = {"m": signal("m_turned", KC), "r": signal("r_turned", 3 * KC)}
        m_full = signal("m_full", KC + 2 * JD + 2 + JD + STEPS)
        xs_ready = signal("xs_ready", JD)
        sz_ready = signal("sz_ready", JD)
        conv_tap = signal("conv_tap", JD * TAPS)
        xc_ready = signal("xc_ready", JD)
        dtr_ready = signal("dtr_ready", 1)
        bcf_ready = signal("bcf_ready", 1)
        bc_split = signal("bc_split", 5)
        sp_abs = signal("sp_abs", JD)
        sp_relu = signal("sp_relu", JD)
        sp_exp = signal("sp_exp", JD)
        sp_u = signal("sp_u", JD)
        sp_rest = signal("sp_rest", JD)
        sp_sum = signal("sp_sum", JD)
        sp_ln = signal("sp_ln", JD)
        dt_ready = signal("dt_ready", JD)
        dtx_ready = signal("dtx_ready", JD)
        b_ready = signal("b_ready", STEPS)
        decay_ready = signal("decay_ready", 2 * STEPS)
        bu_ready = signal("bu_ready", 2 * STEPS)
        scanned = signal("scanned", 2 * STEPS)
        hc_ready = signal("hc_ready", 2 * STEPS)
        y_added = signal("y_added", 2 * STEPS)
        c_full = signal("c_full", STEPS + 2)
        y_read = signal("y_read", JD)
        gated = signal("gated", JD)
        m_done = signal("m_done", 2)
        r_full = signal("r_full", 3 * KC + 2 * FM + 3 * CT)
        v_full = signal("v_full", 2 * FM + 6)
        v_read = signal("v_read", 2 * FM + 6)
        sg_ready = signal("sg_ready", 2 * FM)
        gate_read = signal("gate_read", FM)
        mix_scaled = signal("mix_scaled", 3 * KC)
        mix_ready = signal("mix_ready", 3 * KC)
        recept_ready = signal("recept_ready", CT)
        kb_ready = signal("kb_ready", CT)
        eu_ready = signal("eu_ready", CT)
        vv_ready = signal("vv_ready", CT)
        k_decayed = signal("k_decayed", CT)
        k_clipped = signal("k_clipped", CT)
        e_ready = signal("e_ready", CT)
        eu_clipped = signal("eu_clipped", CT)
        ev_ready = signal("ev_ready", CT)
        euv_ready = signal("euv_ready", CT)
        den_ready = signal("den_ready", CT)
        e_summed = signal("e_summed", CT)
        ev_summed = signal("ev_summed", CT)
        num_ready = signal("num_ready", CT)
        ln_ready = signal("ln_ready", CT)
        rec_ready = signal("rec_ready", CT)
        newton = signal("newton", 3 * CT)
        wkv_ready = signal("wkv_ready", CT)

        def col(name, i):
            return par[:, PC[name] + i:PC[name] + i + 1]

        def channel_tile(s):
            return 2 * (s // (2 * NST)) + s % 2

        def sequences(engine, run):
            run(MAMBA, 0, None)
            with engine.Fori(0, NSEQ - 1) as b:
                run(BOTH, b + 1, b)
            run(REST, None, NSEQ - 1)

        block = ctx.enter_context(nc.Block())

        @block.sync
        def _(sp):
            sp.sem_inc(out_stored.sem, 16)
            sp.dma_start(xin[:, :, :], x_v[0]).then_inc(x_loaded.sem, 16)
            sp.dma_start(par[:, :], params).then_inc(par_in.sem, 16)
            kp = "(k p) n -> p k n"
            sp.dma_start(ident[:, :], ident_in).then_inc(par_in.sem, 16)
            for dst, src in ((win[:, :, :], w_in.rearrange(kp, p=P)),
                             (wx_dt[:, :, :], w_x[:, 0:RANK].rearrange(kp, p=P)),
                             (wx_bc[:, :, 0, :], w_x[:, RANK:].rearrange(kp, p=P)),
                             (wx_bc[:, :, 1, :], w_x[:, RANK:].rearrange(kp, p=P)),
                             (wx_bc[:, :, 2, :], w_x[:, RANK:].rearrange(kp, p=P)),
                             (wdt[:, :], w_dt),
                             (wout[:, :, :], w_out.rearrange(kp, p=P)),
                             (wr[:, :, :], w_r.rearrange(kp, p=P)),
                             (wk[:, :, :], w_k.rearrange(kp, p=P)),
                             (wv[:, :, :], w_v.rearrange(kp, p=P)),
                             (wo[:, :, :], w_o.rearrange(kp, p=P)),
                             (bo[:, :], b_o)):
                sp.dma_start(dst, src).then_inc(weights_in.sem, 16)
            for dst, src in ((wgate, w_gate), (wup, w_up), (wdown, w_down)):
                sp.dma_start(dst[:, :, :].bitcast(i32), src.rearrange(kp, p=P)).then_inc(ffn_in.sem, 16)
            sp.dma_start(t_left[:, :], steps_left.to_broadcast([P, T])).then_inc(ffn_in.sem, 16)

            def reload(m):
                sp.wait_ge(n_turned["m"].sem, at(n_turned["m"], m, KC))
                sp.dma_start(xin[:, :, :], x_v[m]).then_inc(x_loaded.sem, 16)

            reload(0)
            with sp.Fori(0, NSEQ - 1) as b:
                sp.wait_ge(m_done.sem, at(m_done, b, 2))
                sp.dma_start(xin[:, :, :], x_v[b + 1]).then_inc(x_loaded.sem, 16)
                reload(b + 1)
                sp.wait_ge(v_read.sem, at(v_read, b, v_read.per))
                sp.dma_start(out_v[b], xout).then_inc(out_stored.sem, 16)
            sp.wait_ge(v_read.sem, at(v_read, NSEQ - 1, v_read.per))
            sp.dma_start(out_v[NSEQ - 1], xout).then_inc(out_stored.sem, 16)
            sp.wait_ge(out_stored.sem, at(out_stored, NSEQ - 1, 16))

        @block.gpsimd
        def _(pool):
            pool.memset(select[:, :, :], 0.0).then_inc(pool_const.sem, 1)
            pool.memset(minus_half[:, :], -0.5).then_inc(pool_const.sem, 1)
            pool.memset(ones[:, :], 1.0).then_inc(pool_const.sem, 1)
            pool.memset(xs[:, :, 0:TAPS - 1], 0.0).then_inc(pool_const.sem, 1)
            pool.memset(xT[:, :, 0:1], 0.0).then_inc(pool_const.sem, 1)
            pool.memset(xT[:, :, T + 1:T + 2], 0.0).then_inc(pool_const.sem, 1)
            pool.memset(sums[:, :, 0:1], 0.0).then_inc(pool_const.sem, 1)
            pool.wait_ge(pool_const.sem, 7)
            for part in range(3):
                rows = select[2 * NST * part:2 * NST * (part + 1), :, :]
                pool.affine_select(out=rows, in_=rows, compare_op=ALU.not_equal, fill=1.0, base=0,
                                   pattern=[[-1, 2 * NST], [0, P]], channel_multiplier=1)\
                    .then_inc(pool_const.sem, 1)
            pool.wait_ge(pool_const.sem, 10)

            def norm(f, seq, i):
                pool.wait_ge(n_var[f].sem, at(n_var[f], seq, i + 1))
                pool.tensor_tensor(rstd[f][:, :], var_eps[f][:, :], minus_half[:, :], ALU.pow)\
                    .then_inc(n_rstd[f].sem, 1)

            def inputs(m, i):
                pool.wait_ge(b_ready.sem, at(b_ready, m, i + 1))
                for s in (2 * i, 2 * i + 1):
                    if s >= 2:
                        pool.wait_ge(scanned.sem, at(scanned, m, s - 1))
                    pool.tensor_tensor(bu[:, s % 2, :], dtx[:, channel_tile(s), :], b_all[:, i % 3, :],
                                       ALU.mult).then_inc(bu_ready.sem, 1)

            def run(units, m, r):
                for unit, i in units:
                    if unit == "g_rstd_m":
                        norm("m", m, 0)
                    elif unit == "g_rstd_r":
                        norm("r", r, i)
                    elif unit == "g_dtx":
                        pool.wait_ge(dt_ready.sem, at(dt_ready, m, i + 1))
                        pool.tensor_tensor(dtx[:, i, :], dt[:, i, :], xc[:, i, :], ALU.mult)\
                            .then_inc(dtx_ready.sem, 1)
                    elif unit == "m_step":
                        if i == 0:
                            pool.wait_ge(dtx_ready.sem, at(dtx_ready, m, JD))
                            inputs(m, 0)
                        if i + 1 < STEPS:
                            inputs(m, i + 1)
                    elif unit == "g_mix":
                        pool.wait_ge(n_turned["r"].sem, at(n_turned["r"], r, 2 * KC))
                        pool.sem_inc(carried.sem, 1)
                        for k in range(KC):
                            pool.tensor_scalar(mix[:, i, k, :], xT[:, k, 0:T], MIX[i], 1.0, ALU.mult, ALU.mult)\
                                .then_inc(mix_scaled.sem, 1)
                    elif unit == "g_eu":
                        pool.wait_ge(eu_ready.sem, at(eu_ready, r, i + 1))
                        pool.sem_inc(carried.sem, 1)
                        pool.tensor_scalar(den[i % 2], den[i % 2], float(np.exp(np.float32(HI))),
                                           float(np.exp(np.float32(LO))), ALU.min, ALU.max).then_inc(eu_clipped.sem, 1)
                        pool.wait_ge(vv_ready.sem, at(vv_ready, r, i + 1))
                        pool.wait_ge(eu_clipped.sem, at(eu_clipped, r, i + 1))
                        if i >= 2:
                            pool.wait_ge(wkv_ready.sem, at(wkv_ready, r, i - 1))
                        pool.tensor_tensor(num[i % 2], den[i % 2], vv[i % 2], ALU.mult).then_inc(euv_ready.sem, 1)
                    elif unit == "g_ev":
                        pool.wait_ge(e_ready.sem, at(e_ready, r, i + 1))
                        if i:
                            pool.wait_ge(ev_summed.sem, at(ev_summed, r, i))
                        pool.tensor_tensor(ev, ek[i % 2], vv[i % 2], ALU.mult).then_inc(ev_ready.sem, 1)
                    elif unit == "g_den":
                        pool.wait_ge(e_summed.sem, at(e_summed, r, i + 1))
                        pool.wait_ge(euv_ready.sem, at(euv_ready, r, i + 1))
                        pool.tensor_tensor(den[i % 2], sums[:, 0, 0:T], den[i % 2], ALU.add).then_inc(den_ready.sem, 1)

            sequences(pool, run)

        @block.scalar
        def _(act):
            act.wait_ge(par_in.sem, 32)
            a0 = PC["A_log"]
            act.activation(neg_a[:, :], par[:, a0:a0 + JD * NST], ACT.Exp).then_inc(setup_act.sem, 1)
            act.wait_ge(pool_const.sem, 7)
            act.wait_ge(setup_dve.sem, 7)

            def copy_b(m, i, src):
                if i >= 3:
                    act.wait_ge(bu_ready.sem, at(bu_ready, m, 2 * i - 4))
                act.copy(b_all[:, i % 3, :], src[:, :]).then_inc(b_ready.sem, 1)

            def exponentials(m, i):
                for s in (2 * i, 2 * i + 1):
                    j, n = channel_tile(s), i % NST
                    if s >= 4:
                        act.wait_ge(scanned.sem, at(scanned, m, s - 3))
                    act.activation(decay[:, s % 4, :], dt[:, j, :], ACT.Exp,
                                   scale=neg_a[:, j * NST + n:j * NST + n + 1]).then_inc(decay_ready.sem, 1)

            def run(units, m, r):
                mf, rf = [0], [0]

                def from_m():
                    mf[0] += 1
                    act.wait_ge(m_full.sem, at(m_full, m, mf[0]))
                    return ps_m

                def from_r(unit, i, k=0):
                    rf[0] += 1
                    act.wait_ge(r_full.sem, at(r_full, r, rf[0]))
                    return ps_r[R_BANK[unit, i, k]]

                for unit, i in units:
                    if unit == "ma_turn":
                        for k in range(KC):
                            act.copy(xnT[:, k, :], from_m()[:, :]).then_inc(n_turned["m"].sem, 1)
                    elif unit == "a_in":
                        src = from_m()
                        if i < JD:
                            act.copy(xs[:, i, TAPS - 1:], src[:, :]).then_inc(xs_ready.sem, 1)
                        else:
                            act.activation(sz[:, i - JD, :], src[:, :], ACT.Silu).then_inc(sz_ready.sem, 1)
                    elif unit == "a_xc":
                        for j in range(JD):
                            act.wait_ge(conv_tap.sem, at(conv_tap, m, JD * (TAPS - 1) + j + 1))
                            act.activation(xc[:, j, :], xc[:, j, :], ACT.Silu).then_inc(xc_ready.sem, 1)
                    elif unit == "a_xproj":
                        src = from_m()
                        if i == 0:
                            act.copy(bcf, src[0:6 * NST, :]).then_inc(bcf_ready.sem, 1)
                        else:
                            act.copy(dtr, src[0:RANK, :]).then_inc(dtr_ready.sem, 1)
                    elif unit == "a_dt":
                        if i == 0:
                            act.preload_act_table_set("natural_log_exp_and_others")
                        src, bias = from_m(), col("b_dt", i)
                        act.activation(dtx[:, i, :], src[:, :], ACT.Abs, bias=bias).then_inc(sp_abs.sem, 1)
                        act.activation(dt[:, i, :], src[:, :], ACT.Relu, bias=bias).then_inc(sp_relu.sem, 1)
                        act.wait_ge(sp_abs.sem, at(sp_abs, m, i + 1))
                        act.activation(dtx[:, i, :], dtx[:, i, :], ACT.Exp, scale=-1.0).then_inc(sp_exp.sem, 1)
                    elif unit == "a_ln":
                        act.wait_ge(sp_rest.sem, at(sp_rest, m, i + 1))
                        act.activation(u1[:, 0, :], u1[:, 0, :], ACT.Ln).then_inc(sp_ln.sem, 1)
                    elif unit == "m_step":
                        if i == 0:
                            copy_b(m, 0, from_m())
                            copy_b(m, 1, from_m())
                            act.wait_ge(dt_ready.sem, at(dt_ready, m, JD))
                            exponentials(m, 0)
                        if i + 2 < STEPS:
                            copy_b(m, i + 2, from_m())
                        if i + 1 < STEPS:
                            exponentials(m, i + 1)
                    elif unit == "ra_turn":
                        for k in range(KC):
                            act.copy(xT[:, k, 1:T + 1], from_r("rp_turn", i, k)[:, :]).then_inc(n_turned["r"].sem, 1)
                    elif unit == "a_gate":
                        src = from_r("p_gate", i)
                        if i % FM >= 2:
                            act.wait_ge(v_read.sem, at(v_read, r, V_COUNT["v_up", i - 2]))
                        if i < FM:
                            act.activation(sg[:, i % 2, :], src[:, :], ACT.Silu).then_inc(sg_ready.sem, 1)
                        else:
                            act.activation(sg[:, i % 2, :], src[:, :], ACT.Tanh, scale=0.5).then_inc(sg_ready.sem, 1)
                    elif unit == "a_recept":
                        act.activation(yr[:, i, :], from_r("p_recept", i)[:, :], ACT.Tanh, bias=half_br[:, i:i + 1],
                                       scale=0.5).then_inc(recept_ready.sem, 1)
                    elif unit == "a_kv":
                        if i == 0:
                            act.preload_act_table_set("natural_log_exp_and_others")
                            act.wait_ge(out_stored.sem, at(out_stored, r, 0))
                        src = from_r("p_k", i)
                        if i >= 2:
                            act.wait_ge(e_summed.sem, at(e_summed, r, i - 1))
                            act.wait_ge(ev_ready.sem, at(ev_ready, r, i - 1))
                            act.wait_ge(wkv_ready.sem, at(wkv_ready, r, i - 1))
                        act.activation(ek[i % 2], src[:, :], ACT.Identity, bias=col("bk", i)).then_inc(kb_ready.sem, 1)
                        act.activation(den[i % 2], src[:, :], ACT.Exp, bias=ubk[:, i:i + 1]).then_inc(eu_ready.sem, 1)
                        act.activation(vv[i % 2], from_r("p_v", i)[:, :], ACT.Identity, bias=col("bv", i))\
                            .then_inc(vv_ready.sem, 1)
                    elif unit == "a_e":
                        act.wait_ge(k_clipped.sem, at(k_clipped, r, i + 1))
                        act.activation(ek[i % 2], ek[i % 2], ACT.Exp).then_inc(e_ready.sem, 1)
                    elif unit == "a_rec":
                        act.wait_ge(den_ready.sem, at(den_ready, r, i + 1))
                        if i:
                            act.wait_ge(newton.sem, at(newton, r, 3 * i - 1))
                        act.activation(rec[:, :], den[i % 2], ACT.Ln).then_inc(ln_ready.sem, 1)
                        act.wait_ge(ln_ready.sem, at(ln_ready, r, i + 1))
                        act.activation(rec[:, :], rec[:, :], ACT.Exp, scale=-1.0).then_inc(rec_ready.sem, 1)

            sequences(act, run)

        @block.vector
        def _(dve):
            dve.wait_ge(par_in.sem, 32)
            d0, k0, q0 = PC["decay"], PC["bk"], PC["U"]
            dve.tensor_scalar(neg_w[:, :], par[:, d0:d0 + CT], 0.0, -1.0, ALU.max, ALU.mult)\
                .then_inc(setup_dve.sem, 1)
            dve.tensor_tensor(ubk[:, :], par[:, q0:q0 + CT], par[:, k0:k0 + CT], ALU.add).then_inc(setup_dve.sem, 1)
            r0 = PC["br"]
            dve.tensor_scalar(half_br[:, :], par[:, r0:r0 + CT], 0.5, None, ALU.mult).then_inc(setup_dve.sem, 1)
            dve.wait_ge(setup_act.sem, 1)
            dve.tensor_scalar(neg_a[:, :], neg_a[:, :], -1.0, None, ALU.mult).then_inc(setup_dve.sem, 1)
            dve.wait_ge(ffn_in.sem, 64)
            for w in (wgate, wup, wdown):
                dve.tensor_scalar(w[:, :, :], w[:, :, :].bitcast(i32), float(np.float32(1.0 / 127.0)), None, ALU.mult)\
                    .then_inc(setup_dve.sem, 1)
            dve.wait_ge(pool_const.sem, 7)

            def statistics(f, seq, i, src):
                for t in range(TT):
                    dve.bn_stats(stats[f][:, t, :], src[:, t, :]).then_inc(n_stats[f].sem, 1)
                dve.wait_ge(n_stats[f].sem, at(n_stats[f], seq, TT * (i + 1)))
                dve.sem_inc(carried.sem, 1)
                for t in range(TT):
                    dve.bn_aggr(moments[f][:, t, :], stats[f][:, t, :]).then_inc(n_moments[f].sem, 1)
                dve.wait_ge(n_moments[f].sem, at(n_moments[f], seq, TT * (i + 1)))
                dve.tensor_scalar(var_eps[f][:, :], moments[f][:, :, 1], EPS_LN, None, ALU.add)\
                    .then_inc(n_var[f].sem, 1)

            def normalize(f, seq, i, src, dst):
                dve.wait_ge(n_rstd[f].sem, at(n_rstd[f], seq, i + 1))
                for t in range(TT):
                    last = dve.tensor_scalar(dst[:, t, :], src[:, t, :], moments[f][:, t, 0:1], rstd[f][:, t:t + 1],
                                             ALU.subtract, ALU.mult)
                last.then_inc(n_normed[f].sem, 1)

            def times_c(m, s):
                dve.wait_ge(scanned.sem, at(scanned, m, s + 1))
                dve.wait_ge(c_full.sem, at(c_full, m, s // 2 + 1))
                if s >= 4:
                    dve.wait_ge(y_added.sem, at(y_added, m, s - 3))
                dve.tensor_tensor(hc[:, s % 4, :], h[:, s % 3, :], ps_c[s // 2 % 2][:, :], ALU.mult)\
                    .then_inc(hc_ready.sem, 1)

            def run(units, m, r):
                vf = [0]

                def from_v():
                    vf[0] += 1
                    dve.wait_ge(v_full.sem, at(v_full, r, vf[0]))

                def add_residual(src, half, dst):
                    from_v()
                    dve.tensor_tensor(dst[:, 2 * half:2 * half + 2, :].rearrange("p t c -> p (t c)"), src[:, :],
                                      xr[:, 2 * half:2 * half + 2, :].rearrange("p t c -> p (t c)"), ALU.add)\
                        .then_inc(v_read.sem, 1)

                for unit, i in units:
                    if unit == "mv_stats":
                        dve.wait_ge(x_loaded.sem, at(x_loaded, m, 16))
                        statistics("m", m, 0, xin)
                    elif unit == "mv_norm":
                        normalize("m", m, 0, xin, xin)
                    elif unit == "v_conv":
                        for j in range(JD):
                            if i == 0:
                                dve.wait_ge(xs_ready.sem, at(xs_ready, m, j + 1))
                                dve.tensor_scalar(xc[:, j, :], xs[:, j, 0:T], col("conv_w", TAPS * j), col("conv_b", j),
                                                  ALU.mult, ALU.add).then_inc(conv_tap.sem, 1)
                            else:
                                dve.wait_ge(conv_tap.sem, at(conv_tap, m, JD * (i - 1) + j + 1))
                                dve.scalar_tensor_tensor(xc[:, j, :], xs[:, j, i:i + T], col("conv_w", TAPS * j + i),
                                                         xc[:, j, :], ALU.mult, ALU.add).then_inc(conv_tap.sem, 1)
                    elif unit == "v_split":
                        n2, n4, n6 = 2 * NST, 4 * NST, 6 * NST
                        dve.wait_ge(bcf_ready.sem, at(bcf_ready, m, 1))
                        dve.tensor_copy(bc3[:, :], bcf[:, :]).then_inc(bc_split.sem, 1)
                        dve.wait_ge(bc_split.sem, at(bc_split, m, 1))
                        dve.tensor_tensor(bcf[:, :], bcf[:, :], bc3[:, :], ALU.subtract).then_inc(bc_split.sem, 1)
                        dve.wait_ge(bc_split.sem, at(bc_split, m, 2))
                        dve.tensor_copy(bc3[n2:n4, :], bcf[n2:n4, :]).then_inc(bc_split.sem, 1)
                        dve.tensor_copy(bc3[n4:n6, :], bcf[n4:n6, :]).then_inc(bc_split.sem, 1)
                        dve.wait_ge(bc_split.sem, at(bc_split, m, 4))
                        dve.tensor_tensor(bc3[n4:n6, :], bcf[n4:n6, :], bc3[n4:n6, :], ALU.subtract)\
                            .then_inc(bc_split.sem, 1)
                    elif unit == "v_dt":
                        u = u1[:, 0, :]
                        if i == 0:
                            dve.wait_ge(bc_split.sem, at(bc_split, m, 5))
                        else:
                            dve.wait_ge(dt_ready.sem, at(dt_ready, m, i))
                        dve.wait_ge(sp_exp.sem, at(sp_exp, m, i + 1))
                        dve.tensor_scalar(u, dtx[:, i, :], 1.0, None, ALU.add).then_inc(sp_u.sem, 1)
                        dve.wait_ge(sp_u.sem, at(sp_u, m, i + 1))
                        dve.scalar_tensor_tensor(dtx[:, i, :], u, 1.0, dtx[:, i, :], ALU.subtract, ALU.subtract)\
                            .then_inc(sp_rest.sem, 1)
                    elif unit == "v_dtsum":
                        u = u1[:, 0, :]
                        dve.wait_ge(sp_rest.sem, at(sp_rest, m, i + 1))
                        dve.wait_ge(sp_ln.sem, at(sp_ln, m, i + 1))
                        dve.tensor_tensor(u, u, dtx[:, i, :], ALU.subtract).then_inc(sp_sum.sem, 1)
                        dve.wait_ge(sp_sum.sem, at(sp_sum, m, i + 1))
                        dve.wait_ge(sp_relu.sem, at(sp_relu, m, i + 1))
                        dve.tensor_tensor(dt[:, i, :], dt[:, i, :], u, ALU.add).then_inc(dt_ready.sem, 1)
                    elif unit == "m_step":
                        for s in (2 * i, 2 * i + 1):
                            dve.wait_ge(decay_ready.sem, at(decay_ready, m, s + 1))
                            dve.wait_ge(bu_ready.sem, at(bu_ready, m, s + 1))
                            if s >= 3:
                                dve.wait_ge(hc_ready.sem, at(hc_ready, m, s - 2))
                            dve.tensor_tensor_scan(h[:, s % 3, :], decay[:, s % 4, :], bu[:, s % 2, :], 0.0,
                                                   ALU.mult, ALU.add).then_inc(scanned.sem, 1)
                            if s % (2 * NST):
                                times_c(m, s - 1)
                    elif unit == "m_gate":
                        times_c(m, 2 * NST * (i + 1) - 1)
                        for j in (2 * i, 2 * i + 1):
                            dve.wait_ge(y_added.sem, at(y_added, m, 2 * NST * (i + 1) - 1 + j % 2))
                            dve.scalar_tensor_tensor(dtx[:, j, :], xc[:, j, :], col("D", j), ps_y[j % 2][:, :],
                                                     ALU.mult, ALU.add).then_inc(y_read.sem, 1)
                        for j in (2 * i, 2 * i + 1):
                            dve.wait_ge(sz_ready.sem, at(sz_ready, m, j + 1))
                            dve.wait_ge(y_read.sem, at(y_read, m, j + 1))
                            dve.tensor_tensor(dtx[:, j, :], dtx[:, j, :], sz[:, j, :], ALU.mult)\
                                .then_inc(gated.sem, 1)
                    elif unit == "m_post":
                        dve.wait_ge(x_loaded.sem, at(x_loaded, m, 32))
                        if r is not None:
                            dve.wait_ge(v_read.sem, at(v_read, r, v_read.per))
                            dve.sem_inc(carried.sem, 1)
                        for half in range(2):
                            part = slice(2 * half, 2 * half + 2)
                            dve.wait_ge(c_full.sem, at(c_full, m, STEPS + half + 1))
                            dve.tensor_tensor(xr[:, part, :].rearrange("p t c -> p (t c)"), ps_c[half][:, :],
                                              xin[:, part, :].rearrange("p t c -> p (t c)"), ALU.add)\
                                .then_inc(m_done.sem, 1)
                    elif unit == "rv_stats":
                        if i == 0:
                            dve.wait_ge(m_done.sem, at(m_done, r, 2))
                        else:
                            dve.wait_ge(v_read.sem, at(v_read, r, vf[0]))
                        statistics("r", r, i, xr)
                    elif unit == "rv_norm":
                        normalize("r", r, i, xr, xnr)
                    elif unit == "v_up":
                        dve.wait_ge(sg_ready.sem, at(sg_ready, r, i + 1))
                        if i < FM:
                            from_v()
                            dve.tensor_tensor(hf[:, i, :], ps_v[:, :], sg[:, i % 2, :], ALU.mult)\
                                .then_inc(v_read.sem, 1)
                        else:
                            gate = ps_r[R_BANK["p_gate", i, 0]]
                            dve.scalar_tensor_tensor(sg[:, i % 2, :], sg[:, i % 2, :], 1.0, gate[:, :],
                                                     ALU.add, ALU.mult).then_inc(gate_read.sem, 1)
                            dve.wait_ge(gate_read.sem, at(gate_read, r, i - FM + 1))
                            from_v()
                            dve.scalar_tensor_tensor(hf[:, i - FM, :], sg[:, i % 2, :], 0.5, ps_v[:, :],
                                                     ALU.mult, ALU.mult).then_inc(v_read.sem, 1)
                    elif unit in ("v_down", "v_wo"):
                        src = ps_r[R_BANK["p" + unit[1:], i, 0]] if i % 2 else ps_v
                        add_residual(src, i % 2, xout if unit == "v_down" and i >= 2 else xr)
                    elif unit == "v_mix":
                        for k in range(KC):
                            dve.wait_ge(mix_scaled.sem, at(mix_scaled, r, KC * i + k + 1))
                            dve.scalar_tensor_tensor(mix[:, i, k, :], xT[:, k, 2:T + 2], 1.0 - MIX[i],
                                                     mix[:, i, k, :], ALU.mult, ALU.add).then_inc(mix_ready.sem, 1)
                    elif unit == "v_exp":
                        dve.wait_ge(kb_ready.sem, at(kb_ready, r, i + 1))
                        dve.scalar_tensor_tensor(ek[i % 2], t_left[:, :], neg_w[:, i:i + 1], ek[i % 2],
                                                 ALU.mult, ALU.add).then_inc(k_decayed.sem, 1)
                        dve.wait_ge(k_decayed.sem, at(k_decayed, r, i + 1))
                        dve.tensor_scalar(ek[i % 2], ek[i % 2], LO, HI, ALU.max, ALU.min).then_inc(k_clipped.sem, 1)
                    elif unit == "v_esum":
                        dve.wait_ge(e_ready.sem, at(e_ready, r, i + 1))
                        if i:
                            dve.wait_ge(den_ready.sem, at(den_ready, r, i))
                        dve.tensor_tensor_scan(sums[:, 0, 1:], ones[:, 0:1].to_broadcast([P, T]), ek[i % 2], 0.0,
                                               ALU.mult, ALU.add).then_inc(e_summed.sem, 1)
                    elif unit == "v_evsum":
                        dve.wait_ge(ev_ready.sem, at(ev_ready, r, i + 1))
                        if i:
                            dve.wait_ge(num_ready.sem, at(num_ready, r, i))
                        dve.tensor_tensor_scan(sums[:, 1, 1:], ones[:, 0:1].to_broadcast([P, T]), ev, 0.0,
                                               ALU.mult, ALU.add).then_inc(ev_summed.sem, 1)
                        dve.wait_ge(ev_summed.sem, at(ev_summed, r, i + 1))
                        dve.wait_ge(euv_ready.sem, at(euv_ready, r, i + 1))
                        dve.tensor_tensor(num[i % 2], sums[:, 1, 0:T], num[i % 2], ALU.add).then_inc(num_ready.sem, 1)
                    elif unit == "v_wkv":
                        nn, dd = num[i % 2], den[i % 2]
                        dve.wait_ge(rec_ready.sem, at(rec_ready, r, i + 1))
                        dve.tensor_tensor(dd, dd, rec[:, :], ALU.mult).then_inc(newton.sem, 1)
                        dve.wait_ge(newton.sem, at(newton, r, 3 * i + 1))
                        dve.scalar_tensor_tensor(dd, dd, 2.0, rec[:, :], ALU.subtract, ALU.mult)\
                            .then_inc(newton.sem, 1)
                        dve.wait_ge(num_ready.sem, at(num_ready, r, i + 1))
                        dve.wait_ge(newton.sem, at(newton, r, 3 * i + 2))
                        dve.scalar_tensor_tensor(nn, dd, -0.5, nn, ALU.mult, ALU.mult).then_inc(newton.sem, 1)
                        dve.wait_ge(recept_ready.sem, at(recept_ready, r, i + 1))
                        dve.wait_ge(newton.sem, at(newton, r, 3 * i + 3))
                        dve.scalar_tensor_tensor(yr[:, i, :], yr[:, i, :], 1.0, nn, ALU.add, ALU.mult)\
                            .then_inc(wkv_ready.sem, 1)

            sequences(dve, run)

        @block.tensor
        def _(pe):
            pe.wait_ge(par_in.sem, 32)
            pe.wait_ge(weights_in.sem, 12 * 16)
            pe.wait_ge(pool_const.sem, 10)
            pe.wait_ge(setup_dve.sem, 7)

            def turn(src, k, dst, full):
                for t in range(TT):
                    last = pe.transpose(dst[:, P * t:P * (t + 1)], src[:, t, P * k:P * (k + 1)], ident[:, :])
                last.then_inc(full.sem, 1)

            def project(dst, pairs, full):
                for n, (lhs, rhs) in enumerate(pairs):
                    last = pe.matmul(dst, lhs, rhs, start=n == 0, stop=n == len(pairs) - 1)
                last.then_inc(full.sem, 1)

            def to_tokens(dst, half, acts, weights, tiles, full, bias):
                for t in (2 * half, 2 * half + 1):
                    d = dst[:, C * (t % 2):C * (t % 2 + 1)]
                    if bias:
                        pe.matmul(d, ones[0:1, 0:P], bo[:, :], start=True, stop=False)
                    for k in range(tiles):
                        last = pe.matmul(d, acts[:, k, P * t:P * (t + 1)], weights[:, k, :],
                                         start=k == 0 and not bias, stop=k == tiles - 1)
                last.then_inc(full.sem, 1)

            def run(units, m, r):
                m_freed = []

                def to_m(freed, count):
                    if m_freed:
                        pe.wait_ge(m_freed[-1][0].sem, at(m_freed[-1][0], m, m_freed[-1][1]))
                    m_freed.append((freed, count))
                    return ps_m

                def to_r(unit, i, k=0):
                    n = R_ORDER.index((unit, i, k))
                    if n >= 2:
                        u, c, kk = R_ORDER[n - 2]
                        freed, count = {
                            "rp_turn": (n_turned["r"], KC * c + kk + 1), "p_recept": (recept_ready, c + 1),
                            "p_gate": (sg_ready, c + 1) if c < FM else (gate_read, c - FM + 1),
                            "p_k": (eu_ready, c + 1), "p_v": (vv_ready, c + 1),
                            "p_down": (v_read, V_COUNT.get(("v_down", c))), "p_wo": (v_read, V_COUNT.get(("v_wo", c))),
                        }[u]
                        pe.wait_ge(freed.sem, at(freed, r, count))
                    return ps_r[R_BANK[unit, i, k]]

                def to_v(unit, i):
                    n = V_USES.index(("v" + unit[1:], i))
                    if n:
                        pe.wait_ge(v_read.sem, at(v_read, r, V_COUNT[V_USES[n - 1]]))
                    return ps_v

                def spread_b(i):
                    n = i % NST
                    pe.matmul(to_m(b_ready, i + 1)[:, :], select[:, n, :], bc3[:, :], start=True, stop=True)\
                        .then_inc(m_full.sem, 1)

                def spread_c(i):
                    n = i % NST
                    if i >= 2:
                        pe.wait_ge(hc_ready.sem, at(hc_ready, m, 2 * i - 2))
                    pe.matmul(ps_c[i % 2][:, :], select[:, NST + n, :], bc3[:, :], start=True, stop=True)\
                        .then_inc(c_full.sem, 1)

                def add_y(s):
                    n = s // 2 % NST
                    if n == 0 and s >= 2 * NST:
                        pe.wait_ge(y_read.sem, at(y_read, m, channel_tile(s) - 1))
                    pe.wait_ge(hc_ready.sem, at(hc_ready, m, s + 1))
                    pe.matmul(ps_y[s % 2][:, :], ident[:, :], hc[:, s % 4, :], start=n == 0, stop=n == NST - 1)\
                        .then_inc(y_added.sem, 1)

                for unit, i in units:
                    if unit == "mp_turn":
                        pe.wait_ge(n_normed["m"].sem, at(n_normed["m"], m, 1))
                        for k in range(KC):
                            turn(xin, k, to_m(n_turned["m"], k + 1), m_full)
                    elif unit == "p_in":
                        if i == 0:
                            pe.wait_ge(n_turned["m"].sem, at(n_turned["m"], m, KC))
                        dst = to_m(xs_ready, i + 1) if i < JD else to_m(sz_ready, i - JD + 1)
                        project(dst[:, :], [(win[:, k, P * i:P * (i + 1)], xnT[:, k, :]) for k in range(KC)], m_full)
                    elif unit == "p_xproj":
                        if i == 0:
                            pe.wait_ge(xc_ready.sem, at(xc_ready, m, JD))
                            project(to_m(bcf_ready, 1)[0:6 * NST, :],
                                    [(wx_bc[:, j, :, :].rearrange("p a b -> p (a b)"), xc[:, j, :])
                                     for j in range(JD)], m_full)
                        else:
                            project(to_m(dtr_ready, 1)[0:RANK, :],
                                    [(wx_dt[:, j, :], xc[:, j, :]) for j in range(JD)], m_full)
                    elif unit == "p_dt":
                        if i == 0:
                            pe.wait_ge(dtr_ready.sem, at(dtr_ready, m, 1))
                        project(to_m(sp_relu, i + 1)[:, :], [(wdt[:, P * i:P * (i + 1)], dtr)], m_full)
                    elif unit == "m_step":
                        if i == 0:
                            pe.wait_ge(bc_split.sem, at(bc_split, m, 5))
                            spread_b(0)
                            spread_b(1)
                            spread_c(0)
                        if i + 2 < STEPS:
                            spread_b(i + 2)
                        if i + 1 < STEPS:
                            spread_c(i + 1)
                        if i % NST:
                            add_y(2 * i - 2)
                            add_y(2 * i - 1)
                    elif unit == "m_gate":
                        add_y(2 * NST * (i + 1) - 2)
                        add_y(2 * NST * (i + 1) - 1)
                    elif unit == "m_post":
                        pe.wait_ge(gated.sem, at(gated, m, JD))
                        for half in range(2):
                            to_tokens(ps_c[half], half, dtx, wout, JD, c_full, False)
                    elif unit == "rp_turn":
                        pe.wait_ge(n_normed["r"].sem, at(n_normed["r"], r, i + 1))
                        for k in range(KC):
                            turn(xnr, k, to_r("rp_turn", i, k), r_full)
                    elif unit == "p_gate":
                        if i % FM == 0:
                            pe.wait_ge(n_turned["r"].sem, at(n_turned["r"], r, KC if i == 0 else 3 * KC))
                        project(to_r("p_gate", i)[:, :],
                                [(wgate[:, k, P * (i % FM):P * (i % FM + 1)], xT[:, k, 1:T + 1]) for k in range(KC)],
                                r_full)
                    elif unit == "p_up":
                        project(to_v("p_up", i)[:, :],
                                [(wup[:, k, P * (i % FM):P * (i % FM + 1)], xT[:, k, 1:T + 1]) for k in range(KC)],
                                v_full)
                    elif unit == "p_down":
                        pe.wait_ge(v_read.sem, at(v_read, r, V_COUNT["v_up", FM - 1 if i < 2 else 2 * FM - 1]))
                        dst = to_r("p_down", i) if i % 2 else to_v("p_down", i)
                        to_tokens(dst, i % 2, hf, wdown, FM, v_full, False)
                    elif unit == "p_recept":
                        if i == 0:
                            pe.wait_ge(mix_ready.sem, at(mix_ready, r, KC))
                        project(to_r("p_recept", i)[:, :],
                                [(wr[:, k, P * i:P * (i + 1)], mix[:, 0, k, :]) for k in range(KC)], r_full)
                    elif unit == "p_k":
                        if i == 0:
                            pe.wait_ge(mix_ready.sem, at(mix_ready, r, 3 * KC))
                        project(to_r("p_k", i)[:, :],
                                [(wk[:, k, P * i:P * (i + 1)], mix[:, 1, k, :]) for k in range(KC)], r_full)
                    elif unit == "p_v":
                        project(to_r("p_v", i)[:, :],
                                [(wv[:, k, P * i:P * (i + 1)], mix[:, 2, k, :]) for k in range(KC)], r_full)
                    elif unit == "p_wo":
                        if i == 0:
                            pe.wait_ge(wkv_ready.sem, at(wkv_ready, r, CT))
                        dst = to_r("p_wo", i) if i % 2 else to_v("p_wo", i)
                        to_tokens(dst, i % 2, yr, wo, CT, v_full, True)

            sequences(pe, run)


def kernel(**inputs):
    import concourse.bacc as bacc
    from concourse.bass_utils import run_bass_kernel_spmd

    a = {k.replace("L0_attn_", "").replace("L0_", ""): np.asarray(v) for k, v in inputs.items()}

    def tiles(v, n):
        return v.reshape(n, P, -1).transpose(1, 0, 2).reshape(P, -1)

    params = np.concatenate([tiles(a["a_conv_w"], JD), tiles(a["a_conv_b"], JD), tiles(a["a_b_dt"], JD),
                             tiles(a["a_A_log"], JD), tiles(a["a_D_param"], JD), tiles(a["b_br"], CT),
                             tiles(a["b_bk"], CT), tiles(a["b_bv"], CT), tiles(a["b_time_decay"], CT),
                             tiles(a["b_U"], CT)], axis=1)
    arrays = {"x": a["a_x"], "w_in": a["a_W_in"].T, "w_x": a["a_W_x"].T, "w_dt": a["a_W_dt"].T,
              "w_out": a["a_W_out"].T, "w_gate": a["ffn_w_gate"].T, "w_up": a["ffn_w_up"].T,
              "w_down": a["ffn_w_down"].T, "w_r": a["b_Wr"].T, "w_k": a["b_Wk"].T, "w_v": a["b_Wv"].T,
              "w_o": a["b_Wo"].T, "b_o": a["b_bo"].reshape(1, C), "params": params,
              "ident": np.eye(P, dtype=np.float32),
              "steps_left": np.arange(T - 1, -1, -1, dtype=np.float32).reshape(1, T)}
    arrays = {k: np.ascontiguousarray(v) for k, v in arrays.items()}
    nc = bacc.Bacc("TRN2", target_bir_lowering=False, num_devices=1)
    args = [nc.dram_tensor(f"{k}_dram", v.shape, mybir.dt.from_np(v.dtype), kind="ExternalInput").ap()
            for k, v in arrays.items()]
    out = nc.dram_tensor("out_dram", (NSEQ, T, C), mybir.dt.float32, kind="ExternalOutput").ap()
    hybrid_block(nc, *args, out)
    r = run_bass_kernel_spmd(nc, [{f"{k}_dram": v for k, v in arrays.items()}], core_ids=[0])
    return r.results[0]["out_dram"]
```

```python
import numpy as np
import concourse.bass as bass
from concourse import mybir
from contextlib import ExitStack

NSEQ, T, C = 8, 512, 256
DIN, NST, TAPS, RANK = 512, 16, 4, 64
HID = 768
ATT = 1024
P = 128
KC, JD, FM, CT, TT = C // P, DIN // P, HID // P, ATT // P, T // P
EPS_LN = 1e-5
EPS = float(np.exp(-1 / 12))
MIX = (EPS / 2.0, EPS + 0.3 / 11, EPS)
LO, HI = -20.0, 10.0
EXP_MAX = 1e12
PC = {}
_at = 0
for _n, _w in (("conv_w", JD * TAPS), ("conv_b", JD), ("b_dt", JD), ("A_log", JD * NST), ("D", JD),
               ("br", CT), ("bk", CT), ("bv", CT), ("decay", CT), ("U", CT)):
    PC[_n] = _at
    _at += _w
NPAR = _at

STEPS = JD // 2 * NST
BU, HC = 4, 7


def in_time(*timed):
    return sorted((x for part in timed for x in part), key=lambda x: x[0])


def norm(f, i, rstd=2.0, normed=2.736, turned=5.0, copied=6.5):
    return [(0.0, f + "v_stats", i), (rstd, "g_rstd_" + f, i), (normed, f + "v_norm", i),
            (turned, f + "p_turn", i), (copied, f + "a_turn", i)]


def after(units, gap, *then):
    for more in then:
        start = max(x[0] for x in units) + gap
        units = units + [(start + t, u, i) for t, u, i in more]
    return units


def ffn(first, half, every, gate, up, product, downs):
    units = []
    for m in range(FM):
        t = every * m
        units += [(t, "p_gate", first + m), (t + gate, "a_gate", first + m), (t + up, "p_up", first + m),
                  (t + product, "v_up", first + m)]
    return units + [(every * FM + t, u, half + k)
                    for t, (u, k) in zip(downs, (("p_down", 0), ("p_down2", 0), ("p_down", 1), ("v_down", 0),
                                                 ("p_down2", 1), ("v_down", 1)))]


M_HEAD = after(norm("m", 0, 2.0, 3.0, 5.0, 6.5), 1.5,
               [x for m, t in zip(range(2 * JD), (0.0, 2.5, 5.0, 7.5, 10.0, 12.5, 21.0, 23.5))
                for x in ((t, "p_in", m), (t + 1.8, "a_in", m))]
               + [x for j in range(JD) for x in ((2.5 * j + 2.8, "v_conv", j), (2.5 * j + 6.0, "a_xc", j))]
               + [(16.0, "p_xproj", 0), (18.0, "a_xproj", 0), (18.5, "p_xproj", 1), (20.5, "a_xproj", 1),
                  (20.0, "v_split", 0)])
M_DT = [(3.0 * j + t, u, j) for j in range(JD) for t, u in
        ((0.0, "p_dt"), (1.221, "a_dt"), (2.5, "v_dt"), (3.6, "a_ln"), (4.2, "v_dtsum"), (5.5, "g_dtx"))]


def scan(every, step, pair_lag, y_lag, c_lead, gate, last):
    units = []
    for i in range(STEPS):
        t = every * i
        units += [(t, "p_b", i), (t + step, "m_step", i)]
        if pair_lag is None:
            units += [(t + y_lag, "p_y", i)]
        elif i % 2:
            units += [(t + pair_lag, "g_pair", i), (t + y_lag, "p_y", i)]
        if i:
            units += [(t - c_lead, "p_c", i)]
        if i % NST == NST - 1:
            units += [(t + y_lag + gate, "v_gate", i // NST)]
    return units + [(every * STEPS - last, "v_last", 0)]


M_SCAN = scan(3.277, 0.1, 4.98, 6.641, 0.74, 0.142, 0.1)
M_SCAN_ALONE = scan(3.0, 0.1, None, 3.4, 1.0, 0.1, 0.1)

MIXING = after(norm("r", 1, 2.382, 3.0, 5.0, 6.5), 1.0,
               [x for q in range(3) for x in ((1.2 * q, "g_mix", q), (1.2 * q + 1.5, "v_mix", q))])
KV = [(4.4 * (c + t), u, c) for c in range(CT) for t, u in
      ((0.0, "p_k"), (0.25, "p_v"), (0.594, "a_kv"), (0.706, "p_recept"), (1.274, "a_recept"),
       (0.715, "v_exp"), (0.78, "g_eu"), (1.0, "a_e"), (1.271, "g_ev"), (1.3, "v_esum"), (1.468, "g_den"),
       (1.622, "v_evsum"), (1.757, "v_den"), (2.1, "a_rec"), (2.4, "v_wkv"))]
WO = [(0.0, "p_wo", 0), (3.5, "p_wo2", 0), (6.256, "p_wo", 1), (7.5, "v_wo", 0), (10.5, "p_wo2", 1), (14.0, "v_wo", 1)]
EARLY = after(norm("r", 0, 2.0, 3.0, 5.0, 6.5), 0.5,
              ffn(0, 0, 3.4, 3.0, 2.896, 5.561, (3.0, 5.5, 8.0, 9.368, 10.5, 13.5)), MIXING)
LATE = after(KV, 0.596, WO, norm("r", 2, 2.0, 3.0, 5.0, 6.563),
             ffn(FM, 2, 3.4, 3.0, 3.3, 5.0, (3.0, 5.5, 8.0, 8.5, 10.5, 13.5)))


def spread(units, start, end):
    whole = max(x[0] for x in units)
    return [(start + t / whole * (end - start), u, i) for t, u, i in units]


def order(*timed):
    return [(u, i) for _, u, i in in_time(*timed)]


M_EARLY_SPAN, R_EARLY_SPAN = (0.056, 0.95), (0.0, 0.924)
M_DT_SPAN, M_SCAN_SPAN, R_LATE_SPAN = (1.023, 1.22), (1.226, 1.966), (1.029, 1.961)
MAMBA_TIMED, ALONE_TIMED = (spread(M_HEAD, *M_EARLY_SPAN) + spread(M_DT, *M_DT_SPAN) + spread(part, *M_SCAN_SPAN)
                            + [(M_SCAN_SPAN[1] + 0.001, "m_post", 0)] for part in (M_SCAN, M_SCAN_ALONE))
REST_TIMED = spread(EARLY, *R_EARLY_SPAN) + spread(LATE, *R_LATE_SPAN)
MAMBA, REST, BOTH = order(ALONE_TIMED), order(REST_TIMED), order(MAMBA_TIMED, REST_TIMED)

R_UNITS = ("rp_turn", "p_gate", "p_recept", "p_k", "p_v", "p_down", "p_wo")
R_BANK, R_ORDER = {}, []
for _u, _i in REST:
    if _u in R_UNITS and not (_u in ("p_down", "p_wo") and _i % 2 == 0):
        for _k in range(KC if _u == "rp_turn" else 1):
            R_BANK[_u, _i, _k] = len(R_ORDER) % 2
            R_ORDER.append((_u, _i, _k))


V_COUNT = {}
for _u, _i in REST:
    if _u in ("v_up", "v_down", "v_wo"):
        V_COUNT[_u, _i] = len(V_COUNT) + 1
V_USES = [k for k in V_COUNT if k[0] == "v_up" or k[1] % 2 == 0]


class Signal:

    def __init__(self, sem, per, first=0):
        self.sem, self.per, self.first = sem, per, first


def at(signal, seq, count):
    return seq * signal.per + (signal.first + count)


def hybrid_block(nc, x, w_in, w_x, w_dt, w_out, w_gate, w_up, w_down, w_r, w_k, w_v, w_o, b_o, params,
                 ident_in, steps_left, out):
    f32, bf16, i32 = mybir.dt.float32, mybir.dt.bfloat16, mybir.dt.int32
    ALU, ACT = mybir.AluOpType, mybir.ActivationFunctionType
    x_v = x.rearrange("s (t p) c -> s p t c", p=P)
    out_v = out.rearrange("s (t p) c -> s p t c", p=P)

    with ExitStack() as ctx:
        def sb(name, shape, dt=f32):
            return ctx.enter_context(nc.sbuf_tensor(name, shape, dt))

        def bank(name):
            return ctx.enter_context(nc.psum_tensor(name, [P, T], f32))

        def signal(name, per, first=0):
            return Signal(ctx.enter_context(nc.semaphore(name)), per, first)

        win = sb("win", [P, KC, 2 * DIN])
        wx_dt = sb("wx_dt", [P, JD, RANK])
        wx_bc = sb("wx_bc", [P, JD, 3, 2 * NST])
        wdt_bo = sb("wdt_bo", [RANK + 1, DIN])
        wdt, bo = wdt_bo[0:RANK, :], wdt_bo[RANK:RANK + 1, 0:C]
        wout = sb("wout", [P, JD, C])
        wgate = sb("wgate", [P, KC, HID])
        wup = sb("wup", [P, KC, HID])
        wdown = sb("wdown", [P, FM, C])
        wr, wk, wv = (sb(n, [P, KC, ATT]) for n in ("wr", "wk", "wv"))
        wo = sb("wo", [P, CT, C])
        par = sb("par", [P, NPAR])
        neg_a = sb("neg_a", [P, JD * NST])
        neg_w = sb("neg_w", [P, CT])
        ubk = sb("ubk", [P, CT])
        neg_br = sb("neg_br", [P, CT])
        ident = sb("ident", [P, P])
        select = sb("select", [3 * 2 * NST, 2 * NST], bf16)
        t_left = sb("t_left", [P, T])
        ones = sb("ones", [P, P])
        minus_half = sb("minus_half", [P, TT])

        xin = sb("xin", [P, TT, C])
        xs = sb("xs", [P, JD, T + TAPS - 1])
        xc = sb("xc", [P, JD, T])
        sz = sb("sz", [P, JD, T])
        dtx = sb("dtx", [P, JD, T])
        u1 = sb("u1", [P, 1, T])
        bcf = u1[0:3 * 2 * NST, 0, :]
        bc3 = sb("bc3", [3 * 2 * NST, T], bf16)
        b_all = sb("b_all", [P, 3, T])
        decay = sb("decay", [P, 4, T])
        xnT = decay[:, 0:KC, :]
        dtr = b_all[0:RANK, 0, :]
        bu = sb("bu", [P, BU, T])
        h = sb("h", [P, 3, T])
        hc = sb("hc", [P, HC, T])
        dt = xs[:, :, TAPS - 1:]

        xr = sb("xr", [P, TT, C])
        xT = sb("xT", [P, KC, T + 2])
        mix = sb("mix", [P, 3, KC, T])
        hf = mix[:, :, :, :].rearrange("p a k t -> p (a k) t")
        yr = sb("yr", [P, CT, T])
        kv = sb("kv", [P, 4, T])
        x_slots = xin[:, :, :].rearrange("p (a t) c -> p a (t c)", a=2)
        ek = [kv[:, 0, :], x_slots[:, 0, :]]
        vv = [kv[:, 1, :], x_slots[:, 1, :]]
        ev = kv[:, 2, :]
        xnr = kv[:, 0:2, :].rearrange("p a (t c) -> p (a t) c", c=C)
        xout = kv[:, 2:4, :].rearrange("p a (t c) -> p (a t) c", c=C)
        sums = sb("sums", [P, 2, T + 1])
        sg = sums[:, :, 1:]
        num = [sb(n, [P, T])[:, :] for n in ("num0", "num1")]
        den = [sb("den0", [P, T])[:, :], kv[:, 3, :]]
        rec = sb("rec", [P, T])

        stats = {f: sb(f + "_stats", [P, TT, 6]) for f in "mr"}
        moments = {f: sb(f + "_moments", [P, TT, 2]) for f in "mr"}
        var_eps = {f: stats[f][:, 0, 0:TT] for f in "mr"}
        rstd = {f: stats[f][:, 1, 0:TT] for f in "mr"}

        ps_m = bank("ps_m")
        ps_c = [bank(f"ps_c{i}") for i in range(2)]
        ps_y = [bank(f"ps_y{i}") for i in range(2)]
        ps_r = [bank(f"ps_r{i}") for i in range(2)]
        ps_v = bank("ps_v")

        m_weights_in = signal("m_weights_in", 0)
        r_weights_in = signal("r_weights_in", 0)
        par_in = signal("par_in", 0)
        ffn_in = signal("ffn_in", 0)
        pool_const = signal("pool_const", 0)
        setup_act = signal("setup_act", 0)
        setup_dve = signal("setup_dve", 0)
        carried = signal("carried", 0)
        x_loaded = signal("x_loaded", 32)
        out_stored = signal("out_stored", 16, first=16)
        n_stats = {"m": signal("m_stat", TT), "r": signal("r_stat", 3 * TT)}
        n_moments = {"m": signal("m_mom", TT), "r": signal("r_mom", 3 * TT)}
        n_var = {"m": signal("m_var", 1), "r": signal("r_var", 3)}
        n_rstd = {"m": signal("m_rstd_done", 1), "r": signal("r_rstd_done", 3)}
        n_normed = {"m": signal("m_normed", 1), "r": signal("r_normed", 3)}
        n_turned = {"m": signal("m_turned", KC), "r": signal("r_turned", 3 * KC)}
        m_full = signal("m_full", KC + 2 * JD + 2 + JD + STEPS)
        xs_ready = signal("xs_ready", JD)
        sz_ready = signal("sz_ready", JD)
        conv_tap = signal("conv_tap", JD * TAPS)
        xc_ready = signal("xc_ready", JD)
        dtr_ready = signal("dtr_ready", 1)
        bcf_ready = signal("bcf_ready", 1)
        bc_split = signal("bc_split", 5)
        sp_abs = signal("sp_abs", JD)
        sp_relu = signal("sp_relu", JD)
        sp_exp = signal("sp_exp", JD)
        sp_u = signal("sp_u", JD)
        sp_rest = signal("sp_rest", JD)
        sp_sum = signal("sp_sum", JD)
        sp_ln = signal("sp_ln", JD)
        dt_ready = signal("dt_ready", JD)
        dtx_ready = signal("dtx_ready", JD)
        b_ready = signal("b_ready", STEPS)
        decay_ready = signal("decay_ready", 2 * STEPS)
        bu_ready = signal("bu_ready", 2 * STEPS)
        scanned = signal("scanned", 2 * STEPS)
        hc_ready = signal("hc_ready", 2 * STEPS)
        y_added_alone = signal("y_added_alone", 0)
        paired = signal("paired", STEPS, first=-STEPS)
        y_added = signal("y_added", STEPS, first=-STEPS)
        c_full = signal("c_full", STEPS + 2)
        y_read = signal("y_read", JD)
        gated = signal("gated", JD)
        m_done = signal("m_done", 2)
        r_full = signal("r_full", 3 * KC + 2 * FM + 3 * CT)
        v_full = signal("v_full", 2 * FM + 6)
        v_read = signal("v_read", 2 * FM + 6)
        sg_ready = signal("sg_ready", 2 * FM)
        gate_read = signal("gate_read", FM)
        mix_scaled = signal("mix_scaled", 3 * KC)
        mix_ready = signal("mix_ready", 3 * KC)
        recept_ready = signal("recept_ready", CT)
        kb_ready = signal("kb_ready", CT)
        eu_ready = signal("eu_ready", CT)
        vv_ready = signal("vv_ready", CT)
        k_decayed = signal("k_decayed", CT)
        k_clipped = signal("k_clipped", CT)
        e_ready = signal("e_ready", CT)
        eu_clipped = signal("eu_clipped", CT)
        ev_ready = signal("ev_ready", CT)
        euv_ready = signal("euv_ready", CT)
        den_ready = signal("den_ready", CT)
        e_summed = signal("e_summed", CT)
        ev_summed = signal("ev_summed", CT)
        num_ready = signal("num_ready", CT)
        ln_ready = signal("ln_ready", CT)
        rec_ready = signal("rec_ready", CT)
        newton = signal("newton", 2 * CT)
        recept_plus = signal("recept_plus", CT)
        den_gated = signal("den_gated", CT)
        wkv_ready = signal("wkv_ready", CT)

        def col(name, i):
            return par[:, PC[name] + i:PC[name] + i + 1]

        def channel_tile(s):
            return 2 * (s // (2 * NST)) + s % 2

        def pair_count(s):
            return 2 * (s // 4) + s % 2 + 1

        def sequences(engine, run, before_rest=None):
            run(MAMBA, 0, None)
            if before_rest:
                before_rest()
            with engine.Fori(0, NSEQ - 1) as b:
                run(BOTH, b + 1, b)
            run(REST, None, NSEQ - 1)

        block = ctx.enter_context(nc.Block())

        @block.sync
        def _(sp):
            sp.sem_inc(out_stored.sem, 16)
            sp.dma_start(xin[:, :, :], x_v[0]).then_inc(x_loaded.sem, 16)
            sp.dma_start(par[:, :], params).then_inc(par_in.sem, 16)
            kp = "(k p) n -> p k n"
            sp.dma_start(ident[:, :], ident_in).then_inc(par_in.sem, 16)
            for dst, src in ((win[:, :, :], w_in.rearrange(kp, p=P)),
                             (wx_dt[:, :, :], w_x[:, 0:RANK].rearrange(kp, p=P)),
                             (wx_bc[:, :, 0, :], w_x[:, RANK:].rearrange(kp, p=P)),
                             (wx_bc[:, :, 1, :], w_x[:, RANK:].rearrange(kp, p=P)),
                             (wx_bc[:, :, 2, :], w_x[:, RANK:].rearrange(kp, p=P)),
                             (wdt, w_dt),
                             (wout[:, :, :], w_out.rearrange(kp, p=P))):
                sp.dma_start(dst, src).then_inc(m_weights_in.sem, 16)
            for dst, src in ((wr[:, :, :], w_r.rearrange(kp, p=P)),
                             (wk[:, :, :], w_k.rearrange(kp, p=P)),
                             (wv[:, :, :], w_v.rearrange(kp, p=P)),
                             (wo[:, :, :], w_o.rearrange(kp, p=P)),
                             (bo, b_o)):
                sp.dma_start(dst, src).then_inc(r_weights_in.sem, 16)
            for dst, src in ((wgate, w_gate), (wup, w_up), (wdown, w_down)):
                sp.dma_start(dst[:, :, :].bitcast(i32), src.rearrange(kp, p=P)).then_inc(ffn_in.sem, 16)
            sp.dma_start(t_left[:, :], steps_left.to_broadcast([P, T])).then_inc(ffn_in.sem, 16)

            def reload(m, r):
                sp.wait_ge(n_turned["m"].sem, at(n_turned["m"], m, KC))
                if r is not None:
                    sp.wait_ge(wkv_ready.sem, at(wkv_ready, r, CT))
                sp.dma_start(xin[:, :, :], x_v[m]).then_inc(x_loaded.sem, 16)

            reload(0, None)
            with sp.Fori(0, NSEQ - 1) as b:
                sp.wait_ge(m_done.sem, at(m_done, b, 2))
                sp.dma_start(xin[:, :, :], x_v[b + 1]).then_inc(x_loaded.sem, 16)
                reload(b + 1, b)
                sp.wait_ge(v_read.sem, at(v_read, b, v_read.per))
                sp.dma_start(out_v[b], xout).then_inc(out_stored.sem, 16)
            sp.wait_ge(v_read.sem, at(v_read, NSEQ - 1, v_read.per))
            sp.dma_start(out_v[NSEQ - 1], xout).then_inc(out_stored.sem, 16)
            sp.wait_ge(out_stored.sem, at(out_stored, NSEQ - 1, 16))

        @block.gpsimd
        def _(pool):
            pool.memset(select[:, :], 0.0).then_inc(pool_const.sem, 1)
            pool.memset(minus_half[:, :], -0.5).then_inc(pool_const.sem, 1)
            pool.memset(ones[:, :], 1.0).then_inc(pool_const.sem, 1)
            pool.memset(xs[:, :, 0:TAPS - 1], 0.0).then_inc(pool_const.sem, 1)
            pool.memset(xT[:, :, 0:1], 0.0).then_inc(pool_const.sem, 1)
            pool.memset(xT[:, :, T + 1:T + 2], 0.0).then_inc(pool_const.sem, 1)
            pool.memset(sums[:, :, 0:1], 0.0).then_inc(pool_const.sem, 1)
            pool.wait_ge(pool_const.sem, 7)
            for part in range(3):
                rows = select[2 * NST * part:2 * NST * (part + 1), :]
                pool.affine_select(out=rows, in_=rows, compare_op=ALU.not_equal, fill=1.0, base=0,
                                   pattern=[[-1, 2 * NST]], channel_multiplier=1)\
                    .then_inc(pool_const.sem, 1)
            pool.wait_ge(pool_const.sem, 10)

            def norm(f, seq, i):
                pool.wait_ge(n_var[f].sem, at(n_var[f], seq, i + 1))
                pool.tensor_tensor(rstd[f], var_eps[f], minus_half[:, :], ALU.pow)\
                    .then_inc(n_rstd[f].sem, 1)

            def inputs(m, i):
                pool.wait_ge(b_ready.sem, at(b_ready, m, i + 1))
                for s in (2 * i, 2 * i + 1):
                    if s >= BU:
                        pool.wait_ge(scanned.sem, at(scanned, m, s - BU + 1))
                    pool.tensor_tensor(bu[:, s % BU, :], dtx[:, channel_tile(s), :], b_all[:, i % 3, :],
                                       ALU.mult).then_inc(bu_ready.sem, 1)

            def run(units, m, r):
                for unit, i in units:
                    if unit == "g_rstd_m":
                        norm("m", m, 0)
                    elif unit == "g_rstd_r":
                        norm("r", r, i)
                    elif unit == "g_dtx":
                        pool.wait_ge(dt_ready.sem, at(dt_ready, m, i + 1))
                        pool.tensor_tensor(dtx[:, i, :], dt[:, i, :], xc[:, i, :], ALU.mult)\
                            .then_inc(dtx_ready.sem, 1)
                    elif unit == "m_step":
                        if i == 0:
                            pool.wait_ge(dtx_ready.sem, at(dtx_ready, m, JD))
                            inputs(m, 0)
                        if i + 1 < STEPS:
                            inputs(m, i + 1)
                    elif unit == "g_pair":
                        for s in (2 * i, 2 * i + 1):
                            pool.wait_ge(hc_ready.sem, at(hc_ready, m, s + 1))
                            pool.tensor_tensor(hc[:, s % HC, :], hc[:, s % HC, :], hc[:, (s - 2) % HC, :], ALU.add)\
                                .then_inc(paired.sem, 1)
                    elif unit == "g_mix":
                        pool.wait_ge(n_turned["r"].sem, at(n_turned["r"], r, 2 * KC))
                        pool.sem_inc(carried.sem, 1)
                        for k in range(KC):
                            pool.tensor_scalar(mix[:, i, k, :], xT[:, k, 0:T], MIX[i], 1.0, ALU.mult, ALU.mult)\
                                .then_inc(mix_scaled.sem, 1)
                    elif unit == "g_eu":
                        pool.wait_ge(vv_ready.sem, at(vv_ready, r, i + 1))
                        pool.wait_ge(eu_clipped.sem, at(eu_clipped, r, i + 1))
                        if i >= 2:
                            pool.wait_ge(wkv_ready.sem, at(wkv_ready, r, i - 1))
                        pool.tensor_tensor(num[i % 2], den[i % 2], vv[i % 2], ALU.mult).then_inc(euv_ready.sem, 1)
                    elif unit == "g_ev":
                        pool.wait_ge(e_ready.sem, at(e_ready, r, i + 1))
                        if i:
                            pool.wait_ge(ev_summed.sem, at(ev_summed, r, i))
                        pool.tensor_tensor(ev, ek[i % 2], vv[i % 2], ALU.mult).then_inc(ev_ready.sem, 1)
                    elif unit == "g_den":
                        pool.wait_ge(e_summed.sem, at(e_summed, r, i + 1))
                        pool.wait_ge(euv_ready.sem, at(euv_ready, r, i + 1))
                        pool.tensor_tensor(den[i % 2], sums[:, 0, 0:T], den[i % 2], ALU.add).then_inc(den_ready.sem, 1)

            sequences(pool, run)

        @block.scalar
        def _(act):
            act.wait_ge(par_in.sem, 32)
            a0 = PC["A_log"]
            act.activation(neg_a[:, :], par[:, a0:a0 + JD * NST], ACT.Exp).then_inc(setup_act.sem, 1)
            act.wait_ge(pool_const.sem, 7)
            act.wait_ge(setup_dve.sem, 4)

            def copy_b(m, i, src):
                if i >= 3:
                    act.wait_ge(bu_ready.sem, at(bu_ready, m, 2 * i - 4))
                act.copy(b_all[:, i % 3, :], src[:, :]).then_inc(b_ready.sem, 1)

            def exponentials(m, i):
                for s in (2 * i, 2 * i + 1):
                    j, n = channel_tile(s), i % NST
                    if s >= 4:
                        act.wait_ge(scanned.sem, at(scanned, m, s - 3))
                    act.activation(decay[:, s % 4, :], dt[:, j, :], ACT.Exp,
                                   scale=neg_a[:, j * NST + n:j * NST + n + 1]).then_inc(decay_ready.sem, 1)

            def run(units, m, r):
                mf, rf = [0], [0]

                def from_m():
                    mf[0] += 1
                    act.wait_ge(m_full.sem, at(m_full, m, mf[0]))
                    return ps_m

                def from_r(unit, i, k=0):
                    rf[0] += 1
                    act.wait_ge(r_full.sem, at(r_full, r, rf[0]))
                    return ps_r[R_BANK[unit, i, k]]

                for unit, i in units:
                    if unit == "ma_turn":
                        for k in range(KC):
                            act.copy(xnT[:, k, :], from_m()[:, :]).then_inc(n_turned["m"].sem, 1)
                    elif unit == "a_in":
                        src = from_m()
                        if i < JD:
                            act.copy(xs[:, i, TAPS - 1:], src[:, :]).then_inc(xs_ready.sem, 1)
                        else:
                            act.activation(sz[:, i - JD, :], src[:, :], ACT.Silu).then_inc(sz_ready.sem, 1)
                    elif unit == "a_xc":
                        act.wait_ge(conv_tap.sem, at(conv_tap, m, TAPS * (i + 1)))
                        act.activation(xc[:, i, :], xc[:, i, :], ACT.Silu).then_inc(xc_ready.sem, 1)
                    elif unit == "a_xproj":
                        src = from_m()
                        if i == 0:
                            act.copy(bcf, src[0:6 * NST, :]).then_inc(bcf_ready.sem, 1)
                        else:
                            act.copy(dtr, src[0:RANK, :]).then_inc(dtr_ready.sem, 1)
                    elif unit == "a_dt":
                        if i == 0:
                            act.preload_act_table_set("natural_log_exp_and_others")
                        src, bias = from_m(), col("b_dt", i)
                        act.activation(dtx[:, i, :], src[:, :], ACT.Abs, bias=bias).then_inc(sp_abs.sem, 1)
                        act.activation(dt[:, i, :], src[:, :], ACT.Relu, bias=bias).then_inc(sp_relu.sem, 1)
                        act.wait_ge(sp_abs.sem, at(sp_abs, m, i + 1))
                        act.activation(dtx[:, i, :], dtx[:, i, :], ACT.Exp, scale=-1.0).then_inc(sp_exp.sem, 1)
                    elif unit == "a_ln":
                        act.wait_ge(sp_rest.sem, at(sp_rest, m, i + 1))
                        act.activation(u1[:, 0, :], u1[:, 0, :], ACT.Ln).then_inc(sp_ln.sem, 1)
                    elif unit == "m_step":
                        if i == 0:
                            copy_b(m, 0, from_m())
                            copy_b(m, 1, from_m())
                            act.wait_ge(dt_ready.sem, at(dt_ready, m, JD))
                            exponentials(m, 0)
                        if i + 1 < STEPS:
                            exponentials(m, i + 1)
                        if i + 2 < STEPS:
                            copy_b(m, i + 2, from_m())
                    elif unit == "ra_turn":
                        for k in range(KC):
                            act.copy(xT[:, k, 1:T + 1], from_r("rp_turn", i, k)[:, :]).then_inc(n_turned["r"].sem, 1)
                    elif unit == "a_gate":
                        src = from_r("p_gate", i)
                        if i % FM >= 2:
                            act.wait_ge(v_read.sem, at(v_read, r, V_COUNT["v_up", i - 2]))
                        if i < FM:
                            act.activation(sg[:, i % 2, :], src[:, :], ACT.Silu).then_inc(sg_ready.sem, 1)
                        else:
                            act.activation(sg[:, i % 2, :], src[:, :], ACT.Tanh, scale=0.5).then_inc(sg_ready.sem, 1)
                    elif unit == "a_recept":
                        act.activation(yr[:, i, :], from_r("p_recept", i)[:, :], ACT.Exp, bias=neg_br[:, i:i + 1],
                                       scale=-1.0).then_inc(recept_ready.sem, 1)
                    elif unit == "a_kv":
                        if i == 0:
                            act.preload_act_table_set("natural_log_exp_and_others")
                            act.wait_ge(out_stored.sem, at(out_stored, r, 0))
                        src = from_r("p_k", i)
                        if i >= 2:
                            act.wait_ge(e_summed.sem, at(e_summed, r, i - 1))
                            act.wait_ge(ev_ready.sem, at(ev_ready, r, i - 1))
                            act.wait_ge(wkv_ready.sem, at(wkv_ready, r, i - 1))
                        act.activation(ek[i % 2], src[:, :], ACT.Identity, bias=col("bk", i)).then_inc(kb_ready.sem, 1)
                        act.activation(den[i % 2], src[:, :], ACT.Exp, bias=ubk[:, i:i + 1]).then_inc(eu_ready.sem, 1)
                        act.activation(vv[i % 2], from_r("p_v", i)[:, :], ACT.Identity, bias=col("bv", i))\
                            .then_inc(vv_ready.sem, 1)
                    elif unit == "a_e":
                        act.wait_ge(k_clipped.sem, at(k_clipped, r, i + 1))
                        act.activation(ek[i % 2], ek[i % 2], ACT.Exp).then_inc(e_ready.sem, 1)
                    elif unit == "a_rec":
                        act.wait_ge(den_gated.sem, at(den_gated, r, i + 1))
                        if i:
                            act.wait_ge(newton.sem, at(newton, r, 2 * i))
                        act.activation(rec[:, :], den[i % 2], ACT.Ln).then_inc(ln_ready.sem, 1)
                        act.wait_ge(ln_ready.sem, at(ln_ready, r, i + 1))
                        act.activation(rec[:, :], rec[:, :], ACT.Exp, scale=-1.0).then_inc(rec_ready.sem, 1)

            sequences(act, run)

        @block.vector
        def _(dve):
            dve.wait_ge(par_in.sem, 32)
            d0, k0, q0 = PC["decay"], PC["bk"], PC["U"]
            dve.tensor_scalar(neg_w[:, :], par[:, d0:d0 + CT], 0.0, -1.0, ALU.max, ALU.mult)\
                .then_inc(setup_dve.sem, 1)
            dve.tensor_tensor(ubk[:, :], par[:, q0:q0 + CT], par[:, k0:k0 + CT], ALU.add).then_inc(setup_dve.sem, 1)
            r0 = PC["br"]
            dve.tensor_scalar(neg_br[:, :], par[:, r0:r0 + CT], -1.0, None, ALU.mult).then_inc(setup_dve.sem, 1)
            dve.wait_ge(setup_act.sem, 1)
            dve.tensor_scalar(neg_a[:, :], neg_a[:, :], -1.0, None, ALU.mult).then_inc(setup_dve.sem, 1)
            dve.wait_ge(pool_const.sem, 7)

            def statistics(f, seq, i, src):
                for t in range(TT):
                    dve.bn_stats(stats[f][:, t, :], src[:, t, :]).then_inc(n_stats[f].sem, 1)
                dve.wait_ge(n_stats[f].sem, at(n_stats[f], seq, TT * (i + 1)))
                dve.sem_inc(carried.sem, 1)
                for t in range(TT):
                    dve.bn_aggr(moments[f][:, t, :], stats[f][:, t, :]).then_inc(n_moments[f].sem, 1)
                dve.wait_ge(n_moments[f].sem, at(n_moments[f], seq, TT * (i + 1)))
                dve.tensor_scalar(var_eps[f], moments[f][:, :, 1], EPS_LN, None, ALU.add)\
                    .then_inc(n_var[f].sem, 1)

            def normalize(f, seq, i, src, dst):
                dve.wait_ge(n_rstd[f].sem, at(n_rstd[f], seq, i + 1))
                for t in range(TT):
                    last = dve.tensor_scalar(dst[:, t, :], src[:, t, :], moments[f][:, t, 0:1], rstd[f][:, t:t + 1],
                                             ALU.subtract, ALU.mult)
                last.then_inc(n_normed[f].sem, 1)

            def times_c(m, s, alone):
                dve.wait_ge(scanned.sem, at(scanned, m, s + 1))
                dve.wait_ge(c_full.sem, at(c_full, m, s // 2 + 1))
                if s >= HC:
                    t = s - HC
                    if alone:
                        dve.wait_ge(y_added_alone.sem, t + 1)
                    else:
                        freed = y_added if t // 2 % 2 else paired
                        dve.wait_ge(freed.sem, at(freed, m, pair_count(t)))
                dve.tensor_tensor(hc[:, s % HC, :], h[:, s % 3, :], ps_c[s // 2 % 2][:, :], ALU.mult)\
                    .then_inc(hc_ready.sem, 1)

            def run(units, m, r):
                vf = [0]

                def from_v():
                    vf[0] += 1
                    dve.wait_ge(v_full.sem, at(v_full, r, vf[0]))

                def add_residual(src, half, dst):
                    from_v()
                    dve.tensor_tensor(dst[:, 2 * half:2 * half + 2, :].rearrange("p t c -> p (t c)"), src[:, :],
                                      xr[:, 2 * half:2 * half + 2, :].rearrange("p t c -> p (t c)"), ALU.add)\
                        .then_inc(v_read.sem, 1)

                for unit, i in units:
                    if unit == "mv_stats":
                        dve.wait_ge(x_loaded.sem, at(x_loaded, m, 16))
                        statistics("m", m, 0, xin)
                    elif unit == "mv_norm":
                        normalize("m", m, 0, xin, xin)
                    elif unit == "v_conv":
                        dve.wait_ge(xs_ready.sem, at(xs_ready, m, i + 1))
                        dve.tensor_scalar(xc[:, i, :], xs[:, i, 0:T], col("conv_w", TAPS * i), col("conv_b", i),
                                          ALU.mult, ALU.add).then_inc(conv_tap.sem, 1)
                        for tap in range(1, TAPS):
                            dve.wait_ge(conv_tap.sem, at(conv_tap, m, TAPS * i + tap))
                            dve.scalar_tensor_tensor(xc[:, i, :], xs[:, i, tap:tap + T], col("conv_w", TAPS * i + tap),
                                                     xc[:, i, :], ALU.mult, ALU.add).then_inc(conv_tap.sem, 1)
                    elif unit == "v_split":
                        n2, n4, n6 = 2 * NST, 4 * NST, 6 * NST
                        dve.wait_ge(bcf_ready.sem, at(bcf_ready, m, 1))
                        dve.tensor_copy(bc3[:, :], bcf[:, :]).then_inc(bc_split.sem, 1)
                        dve.wait_ge(bc_split.sem, at(bc_split, m, 1))
                        dve.tensor_tensor(bcf[:, :], bcf[:, :], bc3[:, :], ALU.subtract).then_inc(bc_split.sem, 1)
                        dve.wait_ge(bc_split.sem, at(bc_split, m, 2))
                        dve.tensor_copy(bc3[n2:n4, :], bcf[n2:n4, :]).then_inc(bc_split.sem, 1)
                        dve.tensor_copy(bc3[n4:n6, :], bcf[n4:n6, :]).then_inc(bc_split.sem, 1)
                        dve.wait_ge(bc_split.sem, at(bc_split, m, 4))
                        dve.tensor_tensor(bc3[n4:n6, :], bcf[n4:n6, :], bc3[n4:n6, :], ALU.subtract)\
                            .then_inc(bc_split.sem, 1)
                    elif unit == "v_dt":
                        u = u1[:, 0, :]
                        if i == 0:
                            dve.wait_ge(bc_split.sem, at(bc_split, m, 5))
                        else:
                            dve.wait_ge(dt_ready.sem, at(dt_ready, m, i))
                        dve.wait_ge(sp_exp.sem, at(sp_exp, m, i + 1))
                        dve.tensor_scalar(u, dtx[:, i, :], 1.0, None, ALU.add).then_inc(sp_u.sem, 1)
                        dve.wait_ge(sp_u.sem, at(sp_u, m, i + 1))
                        dve.scalar_tensor_tensor(dtx[:, i, :], u, 1.0, dtx[:, i, :], ALU.subtract, ALU.subtract)\
                            .then_inc(sp_rest.sem, 1)
                    elif unit == "v_dtsum":
                        u = u1[:, 0, :]
                        dve.wait_ge(sp_rest.sem, at(sp_rest, m, i + 1))
                        dve.wait_ge(sp_ln.sem, at(sp_ln, m, i + 1))
                        dve.tensor_tensor(u, u, dtx[:, i, :], ALU.subtract).then_inc(sp_sum.sem, 1)
                        dve.wait_ge(sp_sum.sem, at(sp_sum, m, i + 1))
                        dve.wait_ge(sp_relu.sem, at(sp_relu, m, i + 1))
                        dve.tensor_tensor(dt[:, i, :], dt[:, i, :], u, ALU.add).then_inc(dt_ready.sem, 1)
                    elif unit == "m_step":
                        for s in (2 * i, 2 * i + 1):
                            dve.wait_ge(decay_ready.sem, at(decay_ready, m, s + 1))
                            dve.wait_ge(bu_ready.sem, at(bu_ready, m, s + 1))
                            if s >= 3:
                                dve.wait_ge(hc_ready.sem, at(hc_ready, m, s - 2))
                            dve.tensor_tensor_scan(h[:, s % 3, :], decay[:, s % 4, :], bu[:, s % BU, :], 0.0,
                                                   ALU.mult, ALU.add).then_inc(scanned.sem, 1)
                            if s:
                                times_c(m, s - 1, r is None)
                    elif unit == "v_last":
                        times_c(m, 2 * STEPS - 1, r is None)
                    elif unit == "v_gate":
                        for j in (2 * i, 2 * i + 1):
                            if r is None:
                                dve.wait_ge(y_added_alone.sem, 2 * NST * (i + 1) - 1 + j % 2)
                            else:
                                dve.wait_ge(y_added.sem, at(y_added, m, NST * (i + 1) - 1 + j % 2))
                            dve.scalar_tensor_tensor(dtx[:, j, :], xc[:, j, :], col("D", j), ps_y[j % 2][:, :],
                                                     ALU.mult, ALU.add).then_inc(y_read.sem, 1)
                        for j in (2 * i, 2 * i + 1):
                            dve.wait_ge(sz_ready.sem, at(sz_ready, m, j + 1))
                            dve.wait_ge(y_read.sem, at(y_read, m, j + 1))
                            dve.tensor_tensor(dtx[:, j, :], dtx[:, j, :], sz[:, j, :], ALU.mult)\
                                .then_inc(gated.sem, 1)
                    elif unit == "m_post":
                        dve.wait_ge(x_loaded.sem, at(x_loaded, m, 32))
                        if r is not None:
                            dve.wait_ge(v_read.sem, at(v_read, r, v_read.per))
                            dve.sem_inc(carried.sem, 1)
                        for half in range(2):
                            part = slice(2 * half, 2 * half + 2)
                            dve.wait_ge(c_full.sem, at(c_full, m, STEPS + half + 1))
                            dve.tensor_tensor(xr[:, part, :].rearrange("p t c -> p (t c)"), ps_c[half][:, :],
                                              xin[:, part, :].rearrange("p t c -> p (t c)"), ALU.add)\
                                .then_inc(m_done.sem, 1)
                    elif unit == "rv_stats":
                        if i == 0:
                            dve.wait_ge(m_done.sem, at(m_done, r, 2))
                        else:
                            dve.wait_ge(v_read.sem, at(v_read, r, vf[0]))
                        statistics("r", r, i, xr)
                    elif unit == "rv_norm":
                        normalize("r", r, i, xr, xnr)
                    elif unit == "v_up":
                        dve.wait_ge(sg_ready.sem, at(sg_ready, r, i + 1))
                        if i < FM:
                            from_v()
                            dve.tensor_tensor(hf[:, i, :], ps_v[:, :], sg[:, i % 2, :], ALU.mult)\
                                .then_inc(v_read.sem, 1)
                        else:
                            gate = ps_r[R_BANK["p_gate", i, 0]]
                            dve.scalar_tensor_tensor(sg[:, i % 2, :], sg[:, i % 2, :], 1.0, gate[:, :],
                                                     ALU.add, ALU.mult).then_inc(gate_read.sem, 1)
                            dve.wait_ge(gate_read.sem, at(gate_read, r, i - FM + 1))
                            from_v()
                            dve.scalar_tensor_tensor(hf[:, i - FM, :], sg[:, i % 2, :], 0.5, ps_v[:, :],
                                                     ALU.mult, ALU.mult).then_inc(v_read.sem, 1)
                    elif unit in ("v_down", "v_wo"):
                        src = ps_r[R_BANK["p" + unit[1:], i, 0]] if i % 2 else ps_v
                        add_residual(src, i % 2, xout if unit == "v_down" and i >= 2 else xr)
                    elif unit == "v_mix":
                        for k in range(KC):
                            dve.wait_ge(mix_scaled.sem, at(mix_scaled, r, KC * i + k + 1))
                            dve.scalar_tensor_tensor(mix[:, i, k, :], xT[:, k, 2:T + 2], 1.0 - MIX[i],
                                                     mix[:, i, k, :], ALU.mult, ALU.add).then_inc(mix_ready.sem, 1)
                    elif unit == "v_exp":
                        dve.wait_ge(kb_ready.sem, at(kb_ready, r, i + 1))
                        dve.scalar_tensor_tensor(ek[i % 2], t_left[:, :], neg_w[:, i:i + 1], ek[i % 2],
                                                 ALU.mult, ALU.add).then_inc(k_decayed.sem, 1)
                        dve.wait_ge(k_decayed.sem, at(k_decayed, r, i + 1))
                        dve.tensor_scalar(ek[i % 2], ek[i % 2], LO, HI, ALU.max, ALU.min).then_inc(k_clipped.sem, 1)
                        dve.wait_ge(eu_ready.sem, at(eu_ready, r, i + 1))
                        dve.tensor_scalar(den[i % 2], den[i % 2], float(np.exp(np.float32(HI))),
                                          float(np.exp(np.float32(LO))), ALU.min, ALU.max).then_inc(eu_clipped.sem, 1)
                    elif unit == "v_esum":
                        dve.wait_ge(e_ready.sem, at(e_ready, r, i + 1))
                        if i:
                            dve.wait_ge(den_ready.sem, at(den_ready, r, i))
                        dve.tensor_tensor_scan(sums[:, 0, 1:], ones[:, 0:1].to_broadcast([P, T]), ek[i % 2], 0.0,
                                               ALU.mult, ALU.add).then_inc(e_summed.sem, 1)
                    elif unit == "v_evsum":
                        dve.wait_ge(ev_ready.sem, at(ev_ready, r, i + 1))
                        if i:
                            dve.wait_ge(num_ready.sem, at(num_ready, r, i))
                        dve.tensor_tensor_scan(sums[:, 1, 1:], ones[:, 0:1].to_broadcast([P, T]), ev, 0.0,
                                               ALU.mult, ALU.add).then_inc(ev_summed.sem, 1)
                        dve.wait_ge(ev_summed.sem, at(ev_summed, r, i + 1))
                        dve.wait_ge(euv_ready.sem, at(euv_ready, r, i + 1))
                        dve.tensor_tensor(num[i % 2], sums[:, 1, 0:T], num[i % 2], ALU.add).then_inc(num_ready.sem, 1)
                    elif unit == "v_den":
                        dve.wait_ge(recept_ready.sem, at(recept_ready, r, i + 1))
                        dve.tensor_scalar(yr[:, i, :], yr[:, i, :], EXP_MAX, 1.0, ALU.min, ALU.add)\
                            .then_inc(recept_plus.sem, 1)
                        dve.wait_ge(den_ready.sem, at(den_ready, r, i + 1))
                        dve.wait_ge(recept_plus.sem, at(recept_plus, r, i + 1))
                        dve.tensor_tensor(den[i % 2], den[i % 2], yr[:, i, :], ALU.mult).then_inc(den_gated.sem, 1)
                    elif unit == "v_wkv":
                        nn, dd = num[i % 2], den[i % 2]
                        dve.wait_ge(rec_ready.sem, at(rec_ready, r, i + 1))
                        dve.tensor_tensor(dd, dd, rec[:, :], ALU.mult).then_inc(newton.sem, 1)
                        dve.wait_ge(newton.sem, at(newton, r, 2 * i + 1))
                        dve.scalar_tensor_tensor(dd, dd, 2.0, rec[:, :], ALU.subtract, ALU.mult)\
                            .then_inc(newton.sem, 1)
                        dve.wait_ge(num_ready.sem, at(num_ready, r, i + 1))
                        dve.wait_ge(newton.sem, at(newton, r, 2 * i + 2))
                        dve.scalar_tensor_tensor(yr[:, i, :], dd, -1.0, nn, ALU.mult, ALU.mult)\
                            .then_inc(wkv_ready.sem, 1)

            def ffn_weights():
                dve.wait_ge(ffn_in.sem, 64)
                for w in (wgate, wup, wdown):
                    dve.tensor_scalar(w[:, :, :], w[:, :, :].bitcast(i32), float(np.float32(1.0 / 127.0)), None,
                                      ALU.mult).then_inc(setup_dve.sem, 1)

            sequences(dve, run, ffn_weights)

        @block.tensor
        def _(pe):
            pe.wait_ge(par_in.sem, 32)
            pe.wait_ge(m_weights_in.sem, 7 * 16)
            pe.wait_ge(pool_const.sem, 10)

            def rest_weights():
                pe.wait_ge(r_weights_in.sem, 5 * 16)
                pe.wait_ge(setup_dve.sem, 7)

            def turn(src, k, dst, full):
                for t in range(TT):
                    last = pe.transpose(dst[:, P * t:P * (t + 1)], src[:, t, P * k:P * (k + 1)], ident[:, :])
                last.then_inc(full.sem, 1)

            def project(dst, pairs, full):
                for n, (lhs, rhs) in enumerate(pairs):
                    last = pe.matmul(dst, lhs, rhs, start=n == 0, stop=n == len(pairs) - 1)
                last.then_inc(full.sem, 1)

            def to_tokens(dst, t, acts, weights, tiles, full, bias):
                d = dst[:, C * (t % 2):C * (t % 2 + 1)]
                if bias:
                    pe.matmul(d, ones[RANK:RANK + 1, 0:P], bo, start=True, stop=False)
                for k in range(tiles):
                    last = pe.matmul(d, acts[:, k, P * t:P * (t + 1)], weights[:, k, :],
                                     start=k == 0 and not bias, stop=k == tiles - 1)
                if t % 2:
                    last.then_inc(full.sem, 1)

            def run(units, m, r):
                m_freed = []
                dst = {}

                def to_m(freed, count):
                    if m_freed:
                        pe.wait_ge(m_freed[-1][0].sem, at(m_freed[-1][0], m, m_freed[-1][1]))
                    m_freed.append((freed, count))
                    return ps_m

                def to_r(unit, i, k=0):
                    n = R_ORDER.index((unit, i, k))
                    if n >= 2:
                        u, c, kk = R_ORDER[n - 2]
                        freed, count = {
                            "rp_turn": (n_turned["r"], KC * c + kk + 1), "p_recept": (recept_ready, c + 1),
                            "p_gate": (sg_ready, c + 1) if c < FM else (gate_read, c - FM + 1),
                            "p_k": (eu_ready, c + 1), "p_v": (vv_ready, c + 1),
                            "p_down": (v_read, V_COUNT.get(("v_down", c))), "p_wo": (v_read, V_COUNT.get(("v_wo", c))),
                        }[u]
                        pe.wait_ge(freed.sem, at(freed, r, count))
                    return ps_r[R_BANK[unit, i, k]]

                def to_v(unit, i):
                    n = V_USES.index(("v" + unit[1:], i))
                    if n:
                        pe.wait_ge(v_read.sem, at(v_read, r, V_COUNT[V_USES[n - 1]]))
                    return ps_v

                def chosen(row):
                    return select[:, row:row + 1].to_broadcast([3 * 2 * NST, P])

                def spread_b(i):
                    n = i % NST
                    pe.matmul(to_m(b_ready, i + 1)[:, :], chosen(n), bc3[:, :], start=True, stop=True)\
                        .then_inc(m_full.sem, 1)

                def spread_c(i):
                    n = i % NST
                    if i >= 2:
                        pe.wait_ge(hc_ready.sem, at(hc_ready, m, 2 * i - 2))
                    pe.matmul(ps_c[i % 2][:, :], chosen(NST + n), bc3[:, :], start=True, stop=True)\
                        .then_inc(c_full.sem, 1)

                def add_y(s):
                    n, alone = s // 2 % NST, r is None
                    first = n == 0 if alone else n == 1
                    if first and s >= 2 * NST:
                        pe.wait_ge(y_read.sem, at(y_read, m, channel_tile(s) - 1))
                    if alone:
                        pe.wait_ge(hc_ready.sem, s + 1)
                    else:
                        pe.wait_ge(paired.sem, at(paired, m, pair_count(s)))
                    pe.matmul(ps_y[s % 2][:, :], ident[:, :], hc[:, s % HC, :], start=first, stop=n == NST - 1)\
                        .then_inc((y_added_alone if alone else y_added).sem, 1)

                for unit, i in units:
                    if unit == "mp_turn":
                        pe.wait_ge(n_normed["m"].sem, at(n_normed["m"], m, 1))
                        for k in range(KC):
                            turn(xin, k, to_m(n_turned["m"], k + 1), m_full)
                    elif unit == "p_in":
                        if i == 0:
                            pe.wait_ge(n_turned["m"].sem, at(n_turned["m"], m, KC))
                        bank = to_m(xs_ready, i + 1) if i < JD else to_m(sz_ready, i - JD + 1)
                        project(bank[:, :], [(win[:, k, P * i:P * (i + 1)], xnT[:, k, :]) for k in range(KC)], m_full)
                    elif unit == "p_xproj":
                        if i == 0:
                            pe.wait_ge(xc_ready.sem, at(xc_ready, m, JD))
                            project(to_m(bcf_ready, 1)[0:6 * NST, :],
                                    [(wx_bc[:, j, :, :].rearrange("p a b -> p (a b)"), xc[:, j, :])
                                     for j in range(JD)], m_full)
                        else:
                            project(to_m(dtr_ready, 1)[0:RANK, :],
                                    [(wx_dt[:, j, :], xc[:, j, :]) for j in range(JD)], m_full)
                    elif unit == "p_dt":
                        if i == 0:
                            pe.wait_ge(dtr_ready.sem, at(dtr_ready, m, 1))
                        project(to_m(sp_relu, i + 1)[:, :], [(wdt[:, P * i:P * (i + 1)], dtr)], m_full)
                    elif unit == "p_b":
                        if i == 0:
                            pe.wait_ge(bc_split.sem, at(bc_split, m, 5))
                            spread_b(0)
                            spread_b(1)
                            spread_c(0)
                        if i + 2 < STEPS:
                            spread_b(i + 2)
                    elif unit == "p_c":
                        spread_c(i)
                    elif unit == "p_y":
                        add_y(2 * i)
                        add_y(2 * i + 1)
                    elif unit == "m_post":
                        pe.wait_ge(gated.sem, at(gated, m, JD))
                        for t in range(TT):
                            to_tokens(ps_c[t // 2], t, dtx, wout, JD, c_full, False)
                    elif unit == "rp_turn":
                        pe.wait_ge(n_normed["r"].sem, at(n_normed["r"], r, i + 1))
                        for k in range(KC):
                            turn(xnr, k, to_r("rp_turn", i, k), r_full)
                    elif unit == "p_gate":
                        if i % FM == 0:
                            pe.wait_ge(n_turned["r"].sem, at(n_turned["r"], r, KC if i == 0 else 3 * KC))
                        project(to_r("p_gate", i)[:, :],
                                [(wgate[:, k, P * (i % FM):P * (i % FM + 1)], xT[:, k, 1:T + 1]) for k in range(KC)],
                                r_full)
                    elif unit == "p_up":
                        project(to_v("p_up", i)[:, :],
                                [(wup[:, k, P * (i % FM):P * (i % FM + 1)], xT[:, k, 1:T + 1]) for k in range(KC)],
                                v_full)
                    elif unit == "p_down":
                        pe.wait_ge(v_read.sem, at(v_read, r, V_COUNT["v_up", FM - 1 if i < 2 else 2 * FM - 1]))
                        dst[unit] = to_r("p_down", i) if i % 2 else to_v("p_down", i)
                        to_tokens(dst[unit], 2 * (i % 2), hf, wdown, FM, v_full, False)
                    elif unit == "p_down2":
                        to_tokens(dst["p_down"], 2 * (i % 2) + 1, hf, wdown, FM, v_full, False)
                    elif unit == "p_recept":
                        project(to_r("p_recept", i)[:, :],
                                [(wr[:, k, P * i:P * (i + 1)], mix[:, 0, k, :]) for k in range(KC)], r_full)
                    elif unit == "p_k":
                        if i == 0:
                            pe.wait_ge(mix_ready.sem, at(mix_ready, r, 3 * KC))
                        project(to_r("p_k", i)[:, :],
                                [(wk[:, k, P * i:P * (i + 1)], mix[:, 1, k, :]) for k in range(KC)], r_full)
                    elif unit == "p_v":
                        project(to_r("p_v", i)[:, :],
                                [(wv[:, k, P * i:P * (i + 1)], mix[:, 2, k, :]) for k in range(KC)], r_full)
                    elif unit == "p_wo":
                        if i == 0:
                            pe.wait_ge(wkv_ready.sem, at(wkv_ready, r, CT))
                        dst[unit] = to_r("p_wo", i) if i % 2 else to_v("p_wo", i)
                        to_tokens(dst[unit], 2 * (i % 2), yr, wo, CT, v_full, True)
                    elif unit == "p_wo2":
                        to_tokens(dst["p_wo"], 2 * (i % 2) + 1, yr, wo, CT, v_full, True)

            sequences(pe, run, rest_weights)


def kernel(**inputs):
    import concourse.bacc as bacc
    from concourse.bass_utils import run_bass_kernel_spmd

    a = {k.replace("L0_attn_", "").replace("L0_", ""): np.asarray(v) for k, v in inputs.items()}

    def tiles(v, n):
        return v.reshape(n, P, -1).transpose(1, 0, 2).reshape(P, -1)

    params = np.concatenate([tiles(a["a_conv_w"], JD), tiles(a["a_conv_b"], JD), tiles(a["a_b_dt"], JD),
                             tiles(a["a_A_log"], JD), tiles(a["a_D_param"], JD), tiles(a["b_br"], CT),
                             tiles(a["b_bk"], CT), tiles(a["b_bv"], CT), tiles(a["b_time_decay"], CT),
                             tiles(a["b_U"], CT)], axis=1)
    arrays = {"x": a["a_x"], "w_in": a["a_W_in"].T, "w_x": a["a_W_x"].T, "w_dt": a["a_W_dt"].T,
              "w_out": a["a_W_out"].T, "w_gate": a["ffn_w_gate"].T, "w_up": a["ffn_w_up"].T,
              "w_down": a["ffn_w_down"].T, "w_r": a["b_Wr"].T, "w_k": a["b_Wk"].T, "w_v": a["b_Wv"].T,
              "w_o": a["b_Wo"].T, "b_o": a["b_bo"].reshape(1, C), "params": params,
              "ident": np.eye(P, dtype=np.float32),
              "steps_left": np.arange(T - 1, -1, -1, dtype=np.float32).reshape(1, T)}
    arrays = {k: np.ascontiguousarray(v) for k, v in arrays.items()}
    nc = bacc.Bacc("TRN2", target_bir_lowering=False, num_devices=1)
    args = [nc.dram_tensor(f"{k}_dram", v.shape, mybir.dt.from_np(v.dtype), kind="ExternalInput").ap()
            for k, v in arrays.items()]
    out = nc.dram_tensor("out_dram", (NSEQ, T, C), mybir.dt.float32, kind="ExternalOutput").ap()
    hybrid_block(nc, *args, out)
    r = run_bass_kernel_spmd(nc, [{f"{k}_dram": v for k, v in arrays.items()}], core_ids=[0])
    return r.results[0]["out_dram"]
```
